# Optimizing a Trainium2 kernel written in Bass

```python
import numpy as np
import jax
import jax.numpy as jnp

def _softmax(x, axis=-1):
    return jax.nn.softmax(x, axis=axis)

def _gelu(x):
    return jax.nn.gelu(x, approximate=True)

def _silu(x):
    return jax.nn.silu(x)

def _sigmoid(x):
    return jax.nn.sigmoid(x)

def _layernorm(x, axis=-1, eps=1e-05):
    m = jnp.mean(x, axis=axis, keepdims=True)
    v = jnp.var(x, axis=axis, keepdims=True)
    return (x - m) / jnp.sqrt(v + eps)

def _scatter_add(tgt, idx, src, axis=0):
    return tgt.at[idx].add(src)

def _segment_sum(src, seg, n):
    return jax.ops.segment_sum(src, seg, n)
kernel_name = 'mk_decoder_postln_d1_seqx_r8_ea30e3'

def setup_inputs(seed: int=0):
    np.random.seed(seed)
    _w = jnp.asarray

    def _rec_inputs():
        import jax
        import jax.numpy as jnp
        _rk = jax.random.key(seed)
        x = -0.0003929 + 0.9999 * jax.random.normal(jax.random.fold_in(_rk, 1), (2, 256, 256), jnp.float32)
        _lenS = 256 - jax.random.randint(jax.random.fold_in(_rk, 7), (2,), 0, max(1, 256 // 4) + 1, jnp.int32)
        _lenS2 = 512 - jax.random.randint(jax.random.fold_in(_rk, 8), (2,), 0, max(1, 512 // 4) + 1, jnp.int32)
        _ctx_2048P = jax.random.normal(jax.random.fold_in(_rk, 11), (2, 16, 256), jnp.float32)
        _ctx_2048c = jax.random.dirichlet(jax.random.fold_in(_rk, 511), 0.3 * jnp.ones((16,), jnp.float32), (2, 512))
        _ctx_2048t = jnp.einsum('bsk,bkd->bsd', _ctx_2048c, _ctx_2048P)
        _ctx_2048t = _ctx_2048t * jax.lax.rsqrt(jnp.mean(jnp.square(_ctx_2048t)) + 1e-12) * 0.953939
        ctx_2048 = -0.000514642 + 1.00011 * (_ctx_2048t + 0.3 * jax.random.normal(jax.random.fold_in(_rk, 611), (2, 512, 256), jnp.float32))
        _validS = jnp.arange(256)[None, :] < _lenS[:, None]
        _validS2 = jnp.arange(512)[None, :] < _lenS2[:, None]
        _causal = jnp.tril(jnp.ones((256, 256), dtype=bool))
        mask_BxS2_ik0 = jnp.where(jnp.broadcast_to(_validS2[:, :], (2, 512)), 0, 1).astype(jnp.int32)
        return (x, ctx_2048, mask_BxS2_ik0)
    x, ctx_2048, mask_BxS2_ik0 = _rec_inputs()

    def _L0_attn_setup():
        import jax, jax.numpy as jnp
        import numpy as np
        B, S, D = (4, 512, 256)
        IDENTITY_WEIGHT = 0.5
        ROT_DIM = D // 2

        def _layernorm(x, gamma, beta, eps=1e-05):
            mu = jnp.mean(x, axis=-1, keepdims=True)
            var = jnp.var(x, axis=-1, keepdims=True)
            return (x - mu) * jax.lax.rsqrt(var + eps) * gamma + beta

        def _rotary(t, rot_dim, theta=10000.0):
            seq = t.shape[-2]
            inv_freq = 1.0 / theta ** (jnp.arange(0, rot_dim, 2, dtype=jnp.float32) / rot_dim)
            freqs = jnp.arange(seq, dtype=jnp.float32)[:, None] * inv_freq[None, :]
            freqs = jnp.repeat(freqs, 2, axis=-1)
            cos, sin = (jnp.cos(freqs), jnp.sin(freqs))
            t_rot, t_pass = (t[..., :rot_dim], t[..., rot_dim:])
            x1, x2 = (t_rot[..., 0::2], t_rot[..., 1::2])
            rot_half = jnp.stack([-x2, x1], axis=-1).reshape(t_rot.shape)
            return jnp.concatenate([t_rot * cos + rot_half * sin, t_pass], axis=-1)

        def _cos_sim(x):
            return x / jnp.linalg.norm(x, axis=-1, keepdims=True)
        key = jax.random.key(seed)
        ks = jax.random.split(key, 3)
        scale = 0.02
        return {'X': jax.random.normal(ks[0], (B, S, D), jnp.float32), 'W_in': jax.random.normal(ks[1], (D, 3 * D), jnp.float32) * scale, 'b_in': jnp.zeros((3 * D,), jnp.float32), 'W_out': jax.random.normal(ks[2], (D, D), jnp.float32) * scale, 'b_out': jnp.zeros((D,), jnp.float32), 'gamma': jnp.ones((D,), jnp.float32), 'beta': jnp.zeros((D,), jnp.float32)}
    _L0_attn_all = _L0_attn_setup()
    _L0_attn_in = {k: v for k, v in _L0_attn_all.items() if k in ('W_in', 'b_in', 'W_out', 'b_out', 'gamma', 'beta')}
    del _L0_attn_all

    def _L0_xattn_setup():
        import jax, jax.numpy as jnp
        import numpy as np
        import math
        H = 256
        NH = 16
        HD = H // NH
        EPS_LN = 1e-05
        RES_SCALE_MAX = 0.3

        def _nan_clean(x, lim=10000.0):
            return jnp.nan_to_num(x, nan=0.0, posinf=lim, neginf=-lim)
        key = jax.random.key(seed)
        ks = jax.random.split(key, 12)
        B, S, T = (4, 256, 32)
        std = 1.0 / math.sqrt(H)
        return {'hidden_states': jax.random.normal(ks[0], (B, S, H), jnp.float32), 'audio_tokens': jax.random.normal(ks[1], (B, T, H), jnp.float32), 'attention_mask': jax.random.randint(ks[2], (B, T), 0, 2, jnp.int32), 'Wq': jax.random.normal(ks[3], (H, H), jnp.float32) * std, 'bq': jnp.zeros((H,), jnp.float32), 'Wk': jax.random.normal(ks[4], (H, H), jnp.float32) * std, 'bk': jnp.zeros((H,), jnp.float32), 'Wv': jax.random.normal(ks[5], (H, H), jnp.float32) * std, 'bv': jnp.zeros((H,), jnp.float32), 'Wo': jax.random.normal(ks[6], (H, H), jnp.float32) * std, 'bo': jnp.zeros((H,), jnp.float32), 'ln_gamma': jnp.ones((H,), jnp.float32), 'ln_beta': jnp.zeros((H,), jnp.float32), 'residual_scale': jnp.float32(0.05)}
    _L0_xattn_all = _L0_xattn_setup()
    _L0_xattn_in = {k: v for k, v in _L0_xattn_all.items() if k in ('Wq', 'bq', 'Wk', 'bk', 'Wv', 'bv', 'Wo', 'bo', 'ln_gamma', 'ln_beta', 'residual_scale')}
    del _L0_xattn_all

    def _L0_ffn_setup():
        import jax, jax.numpy as jnp
        import numpy as np
        HIDDEN = 256
        INTER = 704
        B, S = (2, 256)

        def _ternary(key, shape):
            return jax.random.randint(key, shape, -1, 2).astype(jnp.float32)
        key = jax.random.key(seed)
        ks = jax.random.split(key, 7)
        x = jax.random.normal(ks[0], (B, S, HIDDEN), dtype=jnp.float32)
        gate_w = _ternary(ks[1], (INTER, HIDDEN))
        up_w = _ternary(ks[2], (INTER, HIDDEN))
        down_w = _ternary(ks[3], (HIDDEN, INTER))
        gate_s = jax.random.uniform(ks[4], (INTER,), minval=0.01, maxval=0.1, dtype=jnp.float32)
        up_s = jax.random.uniform(ks[5], (INTER,), minval=0.01, maxval=0.1, dtype=jnp.float32)
        down_s = jax.random.uniform(ks[6], (HIDDEN,), minval=0.01, maxval=0.1, dtype=jnp.float32)
        return {'x': x, 'gate_w': gate_w, 'up_w': up_w, 'down_w': down_w, 'gate_s': gate_s, 'up_s': up_s, 'down_s': down_s}
    _L0_ffn_all = _L0_ffn_setup()
    _L0_ffn_in = {k: v for k, v in _L0_ffn_all.items() if k in ('gate_w', 'up_w', 'down_w', 'gate_s', 'up_s', 'down_s')}
    del _L0_ffn_all
    return {'x': x, 'ctx_2048': ctx_2048, 'mask_BxS2_ik0': mask_BxS2_ik0, 'L0_attn_W_in': _L0_attn_in['W_in'], 'L0_attn_b_in': _L0_attn_in['b_in'], 'L0_attn_W_out': _L0_attn_in['W_out'], 'L0_attn_b_out': _L0_attn_in['b_out'], 'L0_attn_gamma': _L0_attn_in['gamma'], 'L0_attn_beta': _L0_attn_in['beta'], 'L0_xattn_Wq': _L0_xattn_in['Wq'], 'L0_xattn_bq': _L0_xattn_in['bq'], 'L0_xattn_Wk': _L0_xattn_in['Wk'], 'L0_xattn_bk': _L0_xattn_in['bk'], 'L0_xattn_Wv': _L0_xattn_in['Wv'], 'L0_xattn_bv': _L0_xattn_in['bv'], 'L0_xattn_Wo': _L0_xattn_in['Wo'], 'L0_xattn_bo': _L0_xattn_in['bo'], 'L0_xattn_ln_gamma': _L0_xattn_in['ln_gamma'], 'L0_xattn_ln_beta': _L0_xattn_in['ln_beta'], 'L0_xattn_residual_scale': _L0_xattn_in['residual_scale'], 'L0_ffn_gate_w': _L0_ffn_in['gate_w'], 'L0_ffn_up_w': _L0_ffn_in['up_w'], 'L0_ffn_down_w': _L0_ffn_in['down_w'], 'L0_ffn_gate_s': _L0_ffn_in['gate_s'], 'L0_ffn_up_s': _L0_ffn_in['up_s'], 'L0_ffn_down_s': _L0_ffn_in['down_s']}

def reference(x, ctx_2048, mask_BxS2_ik0, L0_attn_W_in, L0_attn_b_in, L0_attn_W_out, L0_attn_b_out, L0_attn_gamma, L0_attn_beta, L0_xattn_Wq, L0_xattn_bq, L0_xattn_Wk, L0_xattn_bk, L0_xattn_Wv, L0_xattn_bv, L0_xattn_Wo, L0_xattn_bo, L0_xattn_ln_gamma, L0_xattn_ln_beta, L0_xattn_residual_scale, L0_ffn_gate_w, L0_ffn_up_w, L0_ffn_down_w, L0_ffn_gate_s, L0_ffn_up_s, L0_ffn_down_s):
    import jax
    import jax.numpy as jnp

    def _L0_attn_ref(X, W_in, b_in, W_out, b_out, gamma, beta):
        import jax, jax.numpy as jnp
        import numpy as np
        B, S, D = (4, 512, 256)
        IDENTITY_WEIGHT = 0.5
        ROT_DIM = D // 2

        def _layernorm(x, gamma, beta, eps=1e-05):
            mu = jnp.mean(x, axis=-1, keepdims=True)
            var = jnp.var(x, axis=-1, keepdims=True)
            return (x - mu) * jax.lax.rsqrt(var + eps) * gamma + beta

        def _rotary(t, rot_dim, theta=10000.0):
            seq = t.shape[-2]
            inv_freq = 1.0 / theta ** (jnp.arange(0, rot_dim, 2, dtype=jnp.float32) / rot_dim)
            freqs = jnp.arange(seq, dtype=jnp.float32)[:, None] * inv_freq[None, :]
            freqs = jnp.repeat(freqs, 2, axis=-1)
            cos, sin = (jnp.cos(freqs), jnp.sin(freqs))
            t_rot, t_pass = (t[..., :rot_dim], t[..., rot_dim:])
            x1, x2 = (t_rot[..., 0::2], t_rot[..., 1::2])
            rot_half = jnp.stack([-x2, x1], axis=-1).reshape(t_rot.shape)
            return jnp.concatenate([t_rot * cos + rot_half * sin, t_pass], axis=-1)

        def _cos_sim(x):
            return x / jnp.linalg.norm(x, axis=-1, keepdims=True)
        Xn = _layernorm(X, gamma, beta)
        QKV = Xn @ W_in + b_in
        Q, K, V = jnp.split(QKV, 3, axis=-1)
        K = _rotary(K, ROT_DIM)
        V = _rotary(V, ROT_DIM)
        A = jnp.sum(_cos_sim(K) * _cos_sim(V), axis=-2)
        A = (1.0 - IDENTITY_WEIGHT) * A + IDENTITY_WEIGHT
        Y = A[:, None, :] * Q
        Y = Y @ W_out + b_out
        return Y + X

    def _L0_xattn_ref(hidden_states, audio_tokens, attention_mask, Wq, bq, Wk, bk, Wv, bv, Wo, bo, ln_gamma, ln_beta, residual_scale):
        import jax, jax.numpy as jnp
        import numpy as np
        import math
        H = 256
        NH = 16
        HD = H // NH
        EPS_LN = 1e-05
        RES_SCALE_MAX = 0.3

        def _nan_clean(x, lim=10000.0):
            return jnp.nan_to_num(x, nan=0.0, posinf=lim, neginf=-lim)
        B, S, _ = hidden_states.shape
        T = audio_tokens.shape[1]
        hs = _nan_clean(hidden_states).astype(jnp.float32)
        at = _nan_clean(audio_tokens).astype(jnp.float32)

        def proj(x, W, b, L):
            y = x @ W.T + b
            return y.reshape(B, L, NH, HD).transpose(0, 2, 1, 3)
        q = _nan_clean(proj(hs, Wq, bq, S))
        k = _nan_clean(proj(at, Wk, bk, T))
        v = _nan_clean(proj(at, Wv, bv, T))
        scale = max(math.sqrt(HD), 1e-08)
        scores = jnp.einsum('bhsd,bhtd->bhst', q, k) / scale
        scores = jnp.clip(scores, -50.0, 50.0)
        scores = jnp.nan_to_num(scores, nan=0.0, posinf=50.0, neginf=-50.0)
        attend = (attention_mask.astype(jnp.float32) > 0.5)[:, None, None, :]
        scores = jnp.where(attend, scores, -10000.0)
        scores = jnp.clip(scores, -50.0, 50.0)
        probs = jax.nn.softmax(scores, axis=-1)
        probs = jnp.nan_to_num(probs, nan=0.0, posinf=1.0, neginf=0.0)
        probs = probs / (probs.sum(axis=-1, keepdims=True) + 1e-08)
        ctx = jnp.einsum('bhst,bhtd->bhsd', probs, v)
        ctx = ctx.transpose(0, 2, 1, 3).reshape(B, S, H)
        delta = _nan_clean(ctx @ Wo.T + bo)
        rs = jnp.clip(residual_scale, 0.0, RES_SCALE_MAX)
        delta = rs * delta
        mu = delta.mean(axis=-1, keepdims=True)
        var = jnp.mean((delta - mu) ** 2, axis=-1, keepdims=True)
        delta = (delta - mu) / jnp.sqrt(var + EPS_LN) * ln_gamma + ln_beta
        return delta

    def _L0_ffn_ref(x, gate_w, up_w, down_w, gate_s, up_s, down_s):
        import jax, jax.numpy as jnp
        import numpy as np
        HIDDEN = 256
        INTER = 704
        B, S = (2, 256)

        def _ternary(key, shape):
            return jax.random.randint(key, shape, -1, 2).astype(jnp.float32)
        b, s, h = x.shape
        xf = x.reshape(b * s, h)
        g = jnp.einsum('th,ih->ti', xf, gate_w) * gate_s
        u = jnp.einsum('th,ih->ti', xf, up_w) * up_s
        hdn = jax.nn.silu(g) * u
        out = jnp.einsum('ti,hi->th', hdn, down_w) * down_s
        return out.reshape(b, s, -1)
    x = _layernorm(x + _L0_attn_ref(x, L0_attn_W_in, L0_attn_b_in, L0_attn_W_out, L0_attn_b_out, L0_attn_gamma, L0_attn_beta), axis=-1)
    x = _layernorm(x + _L0_xattn_ref(x, ctx_2048, mask_BxS2_ik0, L0_xattn_Wq, L0_xattn_bq, L0_xattn_Wk, L0_xattn_bk, L0_xattn_Wv, L0_xattn_bv, L0_xattn_Wo, L0_xattn_bo, L0_xattn_ln_gamma, L0_xattn_ln_beta, L0_xattn_residual_scale), axis=-1)
    x = _layernorm(x + _L0_ffn_ref(x, L0_ffn_gate_w, L0_ffn_up_w, L0_ffn_down_w, L0_ffn_gate_s, L0_ffn_up_s, L0_ffn_down_s), axis=-1)
    return x

_drawn_inputs = setup_inputs


def setup_inputs(seed=0):
    import zlib

    import numpy as np

    out = dict(_drawn_inputs(seed))
    spreads = {'L0_attn_b_in': (0.0, 0.8),
     'L0_attn_b_out': (0.0, 0.1),
     'L0_attn_gamma': (1.0, 0.6),
     'L0_attn_beta': (0.0, 2.0),
     'L0_xattn_bq': (0.0, 0.1),
     'L0_xattn_bk': (0.0, 2.0),
     'L0_xattn_bv': (0.0, 0.1),
     'L0_xattn_bo': (0.0, 0.1),
     'L0_xattn_ln_gamma': (1.0, 0.2),
     'L0_xattn_ln_beta': (0.0, 0.1)}
    factors = {}
    for name, (base, spread) in spreads.items():
        noise = np.random.default_rng([zlib.crc32(name.encode()), seed]).standard_normal(out[name].shape)
        drawn = base * np.exp(spread * noise) if base else spread * noise
        out[name] = jnp.asarray(drawn.astype(out[name].dtype))
    for name, factor in factors.items():
        out[name] = (out[name] * factor).astype(out[name].dtype)
    return out
```

```python
from contextlib import ExitStack

import numpy as np

import concourse.bass as bass
from concourse import mybir

ALU = mybir.AluOpType
ACT = mybir.ActivationFunctionType
F32 = mybir.dt.float32
BF16 = mybir.dt.bfloat16
I32 = mybir.dt.int32

P = 128
B = 2
S = 256
T = 512
D = 256
ROT = D // 2
DC = D // P
TT = S // P
KT = T // P
NH = 16
HD = D // NH
HG = 4
NG = NH // HG
FC = 6
EPS = 1e-5
SCORE_SCALE = 1.0 / np.sqrt(HD)
E_LOW = float(np.exp(np.float32(-50.0)))
E_HIGH = float(np.exp(np.float32(50.0)))
MASKED = -3.0e38
NE = 4
Q_PARTS = (0, 1, 2, 0, 1, 2, 0, 1)
K_PARTS = (0, 0, 0, 1, 1, 1, 2, 2)

C_GAMMA, C_BETA, C_BIN, C_BQ, C_BK, C_GS, C_US, C_RS = 0, 2, 4, 6, 8, 10, 16, 22
NCOL = 23
R_BKV, R_BOUT, R_BV, R_BO, R_LG, R_LB, R_DS = 0, 512, 768, 1024, 1280, 1536, 1792
NROW = 2048


class Plan:

    def __init__(self, jobs):
        self.at = {}
        self.before = {}
        count = [0] * 8
        last = {}
        for name, banks in jobs:
            count[banks[0]] += 1
            self.at[name] = (banks, count[banks[0]])
            self.before[name] = []
            for k in banks:
                if k in last and last[k] not in self.before[name]:
                    self.before[name].append(last[k])
                last[k] = name


def plan():
    jobs = [
        (("k", 0, 0), [0]), (("k", 0, 1), [1]),
        (("zt", 0), [2]), (("zt", 1), [3]),
        (("kv", 0, 0), [4]), (("kv", 0, 1), [5]), (("aq", 0), [6]),
        (("kv", 1, 0), [7]), (("kv", 1, 1), [0]), (("aq", 1), [1]),
        (("k", 1, 0), [2]), (("a", 0), [3]), (("k", 1, 1), [4]), (("y", 0), [5]),
        (("v", 0, 0), [7]), (("v", 0, 1), [0]),
        (("a", 1), [3]), (("y", 1), [2]),
        (("x1t", 0), [6]), (("v", 1, 0), [4]), (("q", 0), [5]), (("v", 1, 1), [7]),
        (("x1t", 1), [3]), (("q", 1), [1]),
    ]
    for b in range(B):
        steps = NG * KT
        jobs += [(("scores", b, s), [2 * (s % 2), 2 * (s % 2) + 1]) for s in range(2)]
        for s in range(steps):
            if s + 2 < steps:
                jobs.append((("scores", b, s + 2), [2 * (s % 2), 2 * (s % 2) + 1]))
            if s % KT == 0:
                jobs.append((("pv", b, s // KT), [4 + s // KT % 2]))
            g = s // KT - 1
            if g >= 0 and s % KT == 1:
                jobs.append((("pvt", b, g), [6 + g % 2]))
            if g >= 0 and s % KT == 3 and g % 2 == 1:
                jobs.append((("ctxt", b, g // 2), [6 + g % 2]))
            if b == 1 and s == 2:
                jobs.append((("pvt", 0, NG - 1), [7]))
            if b == 1 and s == 4:
                jobs.append((("ctxt", 0, 1), [7]))
            if b == 1 and s == 6:
                jobs.append((("delta", 0), [7]))
            if b == 1 and s == 14:
                jobs.append((("x2t", 0), [7]))
    jobs.append((("pvt", 1, NG - 1), [6]))
    ffn0 = [(("gate", 0, m), [0 + m % 2]) for m in range(3)]
    jobs += [(("gate", 0, 0), [0]), (("up", 0, 0), [2]), (("ctxt", 1, 1), [7]),
             (("gate", 0, 1), [1]), (("delta", 1), [6]), (("up", 0, 1), [3]),
             (("gate", 0, 2), [0]), (("up", 0, 2), [2]), (("down", 0, 0), [4]), (("down", 0, 1), [5]),
             (("x2t", 1), [7]),
             (("gate", 1, 0), [1]), (("up", 1, 0), [3]), (("gate", 1, 1), [0]), (("up", 1, 1), [2]),
             (("gate", 1, 2), [1]), (("up", 1, 2), [3]), (("down", 1, 0), [6]), (("down", 1, 1), [7])]
    return Plan(jobs), [name for name, _ in jobs]


PLAN, ORDER = plan()


def decoder_layer(nc, x, ctx_t, mask_cols, cols, rows, rope_cos, rope_sin, w_in, w_out,
                  wq_t, wk_t, wv_t, wo_t, gate_t, up_t, down_t, out):
    with ExitStack() as stack:
        def sb(name, shape, dt=F32):
            return stack.enter_context(nc.sbuf_tensor(name, shape, dt))

        def sem(name):
            return stack.enter_context(nc.semaphore(name))

        def per_batch(name):
            return [sem(f"{name}{b}") for b in range(B)]

        w_in_sb = sb("w_in_sb", [P, DC, 3 * D])
        w_out_sb = sb("w_out_sb", [P, DC, D])
        wq_sb = sb("wq_sb", [P, DC, D])
        wk_sb = sb("wk_sb", [P, DC, D])
        wv_sb = sb("wv_sb", [P, DC, D])
        wo_sb = sb("wo_sb", [P, DC, D])
        gate_sb = sb("gate_sb", [P, DC, FC * P])
        up_sb = sb("up_sb", [P, DC, FC * P])
        down_sb = sb("down_sb", [P, FC, D])
        col = sb("col", [P, NCOL])
        row = sb("row", [P, NROW])
        cos = sb("cos", [P, TT, ROT])
        sin = sb("sin", [P, TT, ROT])
        mask_sb = sb("mask_sb", [P, B * KT], I32)
        mask_bias = sb("mask_bias", [P, B * KT])
        ident = sb("ident", [P, P])
        power = sb("power", [P, 4])
        res2 = sb("res2", [P, 2])
        x_sb = sb("x_sb", [P, B * TT, D])
        x2b = sb("x2b", [P, B * TT, D])
        stats = sb("stats", [P, B, TT, 6])
        mean_var = sb("mean_var", [P, B, TT, 2])
        var_eps = sb("var_eps", [P, B, TT])
        rstd = sb("rstd", [P, B, TT])
        rstd_rs = sb("rstd_rs", [P, B, TT])
        z = sb("z", [P, B * TT, D])
        z_t = sb("z_t", [P, DC, B * S])
        kv = sb("kv", [P, TT, 2, D])
        turned = sb("turned", [P, TT, 2, ROT])
        crossed = sb("crossed", [P, TT, 2, ROT])
        kv_prod = sb("kv_prod", [P, B, TT, D])
        squares = sb("squares", [P, TT, 2, D], BF16)
        norm_sq = sb("norm_sq", [P, B, TT, 2])
        norm_inv = sb("norm_inv", [P, B, TT, 2])
        pair_inv = sb("pair_inv", [P, B, TT])
        gate_a = sb("gate_a", [P, B, DC])
        aq_t = sb("aq_t", [P, DC, B * S])
        h1 = sb("h1", [P, TT, D])
        x1 = sb("x1", [P, B * TT, D])
        x1b = sb("x1b", [P, B * TT, D])
        x1_t = sb("x1_t", [P, DC, B * S])
        ctx_sb = sb("ctx_sb", [P, DC, B * T])
        k_f = sb("k_f", [P, DC, T])
        k_rest = sb("k_rest", [P, DC, T])
        k_part = [sb(f"k_part{i}", [P, DC, T], BF16) for i in range(3)]
        q_f = sb("q_f", [P, DC, S])
        q_rest = sb("q_rest", [P, DC, S])
        q_part = [sb(f"q_part{i}", [P, DC, S], BF16) for i in range(3)]
        k_stack = sb("k_stack", [P, NH, B * T], BF16)
        q_stack = sb("q_stack", [P, NH, B * S], BF16)
        v_sb = sb("v_sb", [P, B * KT, NH, 32])
        weights = sb("weights", [P, NE, HG, S])
        pv_sb = sb("pv_sb", [P, 2, S])
        total_inv = sb("total_inv", [P, TT, HG])
        ctx_out_t = sb("ctx_out_t", [P, DC, S])
        ctx_out = crossed[:].rearrange("p t a r -> p t (a r)")
        delta = turned[:].rearrange("p t a r -> p t (a r)")
        x2 = x2b[:]
        x2_t = z_t[:]
        silu = k_f[:].rearrange("p c (a s) -> p c a s", a=2)
        hidden = ctx_sb[:].rearrange("p c (f s) -> p (c f) s", s=S)[:, 0:FC]
        final = z[:]

        ps = stack.enter_context(nc.psum_tensor("ps", [P, 8, 512], F32))
        q_scratch = nc.dram_tensor("q_scratch", (B, 3, D, S), BF16, kind="Internal").ap()
        k_scratch = nc.dram_tensor("k_scratch", (B, 3, D, T), BF16, kind="Internal").ap()

        loaded = {n: sem(f"loaded_{n}") for n in
                  ("x", "col", "row", "cos", "sin", "mask", "ctx0", "ctx1", "wk", "wv", "w_in", "w_out",
                   "wq", "wo", "gate", "up", "down")}
        bank_filled = [sem(f"bank_filled{k}") for k in range(8)]
        bank_taken = [sem(f"bank_taken{k}") for k in range(8)]
        const_ready = sem("const_ready")
        ident_ready = sem("ident_ready")
        mask_ready = sem("mask_ready")
        res_ready = sem("res_ready")
        v_ones = sem("v_ones")
        x2b_ready = sem("x2b_ready")
        var_ready = sem("var_ready")
        rstd_ready = sem("rstd_ready")
        dve_step = sem("dve_step")
        pool_step = sem("pool_step")
        z_ready = per_batch("z_ready")
        crossed_ready = per_batch("crossed_ready")
        prod_ready = per_batch("prod_ready")
        norms_ready, pair_ready = per_batch("norms_ready"), per_batch("pair_ready")
        x1_ready, x1b_ready, x2_ready = per_batch("x1_ready"), per_batch("x1b_ready"), per_batch("x2_ready")
        kpart_ready, krest_ready = per_batch("kpart_ready"), per_batch("krest_ready")
        k3_ready = per_batch("k3_ready")
        qpart_ready = per_batch("qpart_ready")
        k_stored = [[sem(f"k_stored{b}{i}") for i in range(3)] for b in range(B)]
        q_stored = [[sem(f"q_stored{b}{i}") for i in range(3)] for b in range(B)]
        k_stacked, q_stacked = per_batch("k_stacked"), per_batch("q_stacked")
        clipped = sem("clipped")
        weights_used = sem("weights_used")
        final_ready = sem("final_ready")
        stored = sem("stored")

        def filled(*job):
            banks, n = PLAN.at[job]
            return bank_filled[banks[0]], n

        def taken(*job):
            banks, n = PLAN.at[job]
            return bank_taken[banks[0]], n

        def bank(*job):
            return PLAN.at[job][0][0]

        def full(*job):
            return bank_filled[bank(*job)], 1

        def take(*job):
            return bank_taken[bank(*job)], 1

        STEPS = NG * KT

        def used(n):
            if n % KT == KT - 1:
                return filled("pv", *divmod(n // KT, NG))
            return weights_used, n - n // KT + 1

        def exp_of(b, s):
            return b * STEPS + s + 1

        block = stack.enter_context(nc.Block())

        @block.sync
        def _(sp):
            def by_chunk(a):
                return a.rearrange("(c p) n -> p c n", p=P)

            sp.dma_start(x_sb[:], x.rearrange("(t p) d -> p t d", p=P)).then_inc(loaded["x"], 16)
            sp.dma_start(wk_sb[:], by_chunk(wk_t)).then_inc(loaded["wk"], 16)
            sp.dma_start(ctx_sb[:, :, 0:T], by_chunk(ctx_t)[:, :, 0:T]).then_inc(loaded["ctx0"], 16)
            sp.dma_start(w_in_sb[:], by_chunk(w_in)).then_inc(loaded["w_in"], 16)
            sp.dma_start(row[:], rows.to_broadcast([P, NROW])).then_inc(loaded["row"], 16)
            sp.dma_start(cos[:], rope_cos.rearrange("(t p) d -> p t d", p=P)).then_inc(loaded["cos"], 16)
            sp.dma_start(sin[:], rope_sin.rearrange("(t p) d -> p t d", p=P)).then_inc(loaded["sin"], 16)
            sp.dma_start(ctx_sb[:, :, T:], by_chunk(ctx_t)[:, :, T:]).then_inc(loaded["ctx1"], 16)
            sp.dma_start(w_out_sb[:], by_chunk(w_out)).then_inc(loaded["w_out"], 16)
            sp.dma_start(wv_sb[:], by_chunk(wv_t)).then_inc(loaded["wv"], 16)
            sp.dma_start(wq_sb[:], by_chunk(wq_t)).then_inc(loaded["wq"], 16)

            def store_parts(scratch, part, ready, stored_, b):
                for i in range(3):
                    sp.wait_ge(*ready[i])
                    sp.dma_start(scratch[b, i].rearrange("(c p) t -> p c t", p=P), part[i][:]).then_inc(stored_[b][i], 16)

            def stack_up(scratch, parts, stack_sb, width, stored_, stacked, b):
                for n, i in enumerate(parts):
                    sp.wait_ge(stored_[b][i], 16)
                    sp.dma_start(stack_sb[HD * n:HD * (n + 1), :, b * width:(b + 1) * width],
                                 scratch[b, i].rearrange("(h d) t -> d h t", d=HD)).then_inc(stacked[b], 16)

            def move_k(b):
                store_parts(k_scratch, k_part, [(kpart_ready[b], 2), (kpart_ready[b], 4), (k3_ready[b], 1)],
                            k_stored, b)
                stack_up(k_scratch, K_PARTS, k_stack, T, k_stored, k_stacked, b)

            def move_q(b):
                store_parts(q_scratch, q_part, [(qpart_ready[b], 1), (qpart_ready[b], 2), (qpart_ready[b], 3)],
                            q_stored, b)
                stack_up(q_scratch, Q_PARTS, q_stack, S, q_stored, q_stacked, b)

            move_k(0)
            sp.dma_start(wo_sb[:], by_chunk(wo_t)).then_inc(loaded["wo"], 16)
            move_k(1)
            move_q(0)
            move_q(1)
            sp.dma_start(gate_sb[:], by_chunk(gate_t)).then_inc(loaded["gate"], 16)
            sp.dma_start(up_sb[:], by_chunk(up_t)).then_inc(loaded["up"], 16)
            sp.dma_start(down_sb[:], by_chunk(down_t)).then_inc(loaded["down"], 16)
            for n in range(B * TT):
                sp.wait_ge(final_ready, n + 1)
                sp.dma_start(out[n * P:(n + 1) * P, :], final[:, n, :]).then_inc(stored, 16)
            sp.wait_ge(stored, 16 * B * TT)

        @block.gpsimd
        def _(pool):
            steps = [0]

            def link(ins):
                steps[0] += 1
                ins.then_inc(pool_step, 1)
                pool.wait_ge(pool_step, steps[0])

            nc.gpsimd.memset(power[:], -0.5).then_inc(const_ready, 1)
            link(nc.gpsimd.memset(ident[:], 0.0))
            nc.gpsimd.affine_select(out=ident[:], in_=ident[:], compare_op=ALU.not_equal, fill=1.0, base=0,
                                    pattern=[[-1, P]], channel_multiplier=1).then_inc(ident_ready, 1)
            nc.gpsimd.memset(v_sb[:, 0:KT], 1.0).then_inc(v_ones, 1)
            nc.gpsimd.memset(v_sb[:, KT:2 * KT], 1.0).then_inc(v_ones, 1)
            pool.wait_ge(const_ready, 1)

            uses = [0]

            def inverse_root(b):
                uses[0] += 1
                pool.wait_ge(var_ready, uses[0])
                nc.gpsimd.tensor_tensor(rstd[:, b, :], var_eps[:, b, :], power[:, 0:TT], ALU.pow).then_inc(rstd_ready, 1)

            inverse_root(0)
            inverse_root(1)

            pool.wait_ge(loaded["x"], 16)
            link(nc.gpsimd.tensor_tensor(x2b[:], x_sb[:], x_sb[:], ALU.add))
            pool.wait_ge(loaded["row"], 16)

            def add_b_out(b):
                nc.gpsimd.tensor_tensor(x2b[:, TT * b:TT * (b + 1)], x2b[:, TT * b:TT * (b + 1)],
                                        row[:, R_BOUT:R_BOUT + D].unsqueeze(1).to_broadcast([P, TT, D]),
                                        ALU.add).then_inc(x2b_ready, 1)

            def k_remainder(b, n):
                pool.wait_ge(kpart_ready[b], 2 * n + 2)
                if n == 0:
                    pool.wait_ge(*taken("k", b, 0))
                    pool.wait_ge(*taken("k", b, 1))
                    nc.gpsimd.tensor_tensor(k_rest[:], k_f[:], k_part[0][:], ALU.subtract).then_inc(krest_ready[b], 1)
                else:
                    pool.wait_ge(krest_ready[b], 1)
                    if b > 0:
                        pool.wait_ge(k_stored[b - 1][2], 16)
                    nc.gpsimd.tensor_tensor(k_part[2][:], k_rest[:], k_part[1][:], ALU.subtract).then_inc(k3_ready[b], 1)

            def cross_terms(b):
                pool.wait_ge(loaded["sin"], 16)
                pool.wait_ge(*taken("kv", b, 0))
                pool.wait_ge(*taken("kv", b, 1))
                if b > 0:
                    pool.wait_ge(prod_ready[b - 1], 2)
                for odd in range(2):
                    for t in range(TT):
                        last = nc.gpsimd.tensor_tensor(
                            crossed[:, t, :, odd::2], kv[:, t, :, 1 - odd:ROT:2],
                            sin[:, t, odd::2].unsqueeze(1).to_broadcast([P, 2, ROT // 2]), ALU.mult)
                last.then_inc(crossed_ready[b], 1)

            def norms(b):
                pool.wait_ge(norms_ready[b], 2 * TT)
                link(nc.gpsimd.tensor_tensor(norm_inv[:, b], norm_sq[:, b], power[:, 0:4].rearrange("p (a c) -> p a c", a=2), ALU.pow))
                nc.gpsimd.tensor_tensor(pair_inv[:, b], norm_inv[:, b, :, 0], norm_inv[:, b, :, 1], ALU.mult).then_inc(pair_ready[b], 1)

            k_remainder(0, 0)
            add_b_out(0)
            k_remainder(0, 1)
            cross_terms(0)
            norms(0)
            add_b_out(1)
            cross_terms(1)
            norms(1)
            k_remainder(1, 0)
            inverse_root(0)
            k_remainder(1, 1)
            inverse_root(1)
            for b in range(B):
                pool.wait_ge(x1_ready[b], 2)
                nc.gpsimd.tensor_tensor(x1b[:, TT * b:TT * (b + 1)], x1[:, TT * b:TT * (b + 1)],
                                        row[:, R_LB:R_LB + D].unsqueeze(1).to_broadcast([P, TT, D]),
                                        ALU.add).then_inc(x1b_ready[b], 1)
            pool.wait_ge(res_ready, 2)

            def after_cross(b):
                uses[0] += 1
                pool.wait_ge(var_ready, uses[0])
                link(nc.gpsimd.tensor_tensor(rstd[:, b, :], var_eps[:, b, :], power[:, 0:TT], ALU.pow))
                nc.gpsimd.tensor_tensor(rstd_rs[:, b, :], rstd[:, b, :],
                                        res2[:, 0:1].to_broadcast([P, TT]), ALU.mult).then_inc(rstd_ready, 1)

            after_cross(0)
            inverse_root(0)
            after_cross(1)
            inverse_root(1)
            inverse_root(0)
            for t in range(TT):
                uses[0] += 1
                pool.wait_ge(var_ready, uses[0])
                nc.gpsimd.tensor_tensor(rstd[:, 1, t:t + 1], var_eps[:, 1, t:t + 1], power[:, 0:1], ALU.pow).then_inc(rstd_ready, 1)

        @block.scalar
        def _(act):
            act.dma_start(col[:], cols).then_inc(loaded["col"], 16)
            act.dma_start(mask_sb[:], mask_cols).then_inc(loaded["mask"], 16)

            def k_bias(b, c):
                act.wait_ge(*filled("k", b, c))
                if b > 0:
                    act.wait_ge(krest_ready[b - 1], 1)
                nc.scalar.activation(k_f[:, c, :], ps[:, bank("k", b, c), :], ACT.Identity,
                                     bias=col[:, C_BK + c:C_BK + c + 1]).then_inc(*take("k", b, c))
                act.wait_ge(*taken("k", b, c))
                if b > 0:
                    act.wait_ge(k_stored[b - 1][0], 16)
                nc.scalar.activation(k_part[0][:, c, :], k_f[:, c, :], ACT.Copy).then_inc(kpart_ready[b], 1)

            def k_second(b):
                act.wait_ge(krest_ready[b], 1)
                if b > 0:
                    act.wait_ge(k_stored[b - 1][1], 16)
                    act.wait_ge(k3_ready[b - 1], 1)
                for c in range(DC):
                    nc.scalar.activation(k_part[1][:, c, :], k_rest[:, c, :], ACT.Copy).then_inc(kpart_ready[b], 1)

            def z_scale(b):
                act.wait_ge(*filled("zt", b))
                for c in range(DC):
                    last = nc.scalar.activation(z_t[:, c, S * b:S * (b + 1)], ps[:, bank("zt", b), S * c:S * (c + 1)],
                                                ACT.Identity, scale=col[:, C_GAMMA + c:C_GAMMA + c + 1],
                                                bias=col[:, C_BETA + c:C_BETA + c + 1])
                last.then_inc(*take("zt", b))

            def square_norms(b):
                if b > 0:
                    act.wait_ge(norms_ready[b - 1], 2 * TT)
                for t in range(TT):
                    act.wait_ge(*taken("kv", b, t))
                    for n in range(2):
                        nc.scalar.activation(squares[:, t, n, :], kv[:, t, n, :], ACT.Square,
                                             accum_out=norm_sq[:, b, t, n:n + 1]).then_inc(norms_ready[b], 1)

            act.wait_ge(loaded["col"], 16)
            k_bias(0, 0)
            k_bias(0, 1)
            z_scale(0)
            z_scale(1)
            k_second(0)
            square_norms(0)
            square_norms(1)
            k_bias(1, 0)
            k_bias(1, 1)

            def copy_t(job, b, dst):
                act.wait_ge(*filled(job, b))
                nc.scalar.activation(dst[:, :, S * b:S * (b + 1)],
                                     ps[:, bank(job, b), :].rearrange("p (c s) -> p c s", c=DC), ACT.Copy).then_inc(*take(job, b))

            def q_bias(b):
                act.wait_ge(*filled("q", b))
                if b > 0:
                    act.wait_ge(qpart_ready[b - 1], 3)
                for c in range(DC):
                    last = nc.scalar.activation(q_f[:, c, :], ps[:, bank("q", b), S * c:S * (c + 1)], ACT.Identity,
                                         bias=col[:, C_BQ + c:C_BQ + c + 1])
                last.then_inc(*take("q", b))

            k_second(1)
            copy_t("x1t", 0, x1_t)
            q_bias(0)
            copy_t("x1t", 1, x1_t)
            q_bias(1)

            act.wait_ge(mask_ready, 1)
            for b in range(B):
                for s in range(STEPS):
                    kt = s % KT
                    e = exp_of(b, s)
                    act.wait_ge(*filled("scores", b, s))
                    if e > NE:
                        act.wait_ge(*used(e - NE - 1))
                    k0 = bank("scores", b, s)
                    nc.scalar.activation(weights[:, (e - 1) % NE], ps[:, k0:k0 + 2, :].rearrange("p a (h s) -> p (a h) s", h=2),
                                         ACT.Exp, scale=SCORE_SCALE,
                                         bias=mask_bias[:, b * KT + kt:b * KT + kt + 1]).then_inc(*take("scores", b, s))
                    if b == 1 and s == 15:
                        copy_t("x2t", 0, x2_t)

            pair = [0]

            def silus(b, m):
                act.wait_ge(*filled("gate", b, m))
                pair[0] += 1
                if pair[0] > 2:
                    before = pair[0] - 3
                    act.wait_ge(*taken("up", before // (FC // 2), before % (FC // 2)))
                for i in range(2):
                    last = nc.scalar.activation(silu[:, (pair[0] - 1) % 2, i, :], ps[:, bank("gate", b, m), S * i:S * (i + 1)], ACT.Silu,
                                         scale=col[:, C_GS + 2 * m + i:C_GS + 2 * m + i + 1])
                last.then_inc(*take("gate", b, m))

            for m in range(FC // 2):
                silus(0, m)
            copy_t("x2t", 1, x2_t)
            for m in range(FC // 2):
                silus(1, m)

        @block.vector
        def _(dve):
            steps = [0]

            def link(ins):
                steps[0] += 1
                ins.then_inc(dve_step, 1)
                dve.wait_ge(dve_step, steps[0])

            roots = [0]

            def row_of(start, width=D):
                return row[:, start:start + width].unsqueeze(1).to_broadcast([P, TT, width])

            def moments(b, src, scale=None, eps=EPS, tiles=range(TT)):
                tiles = list(tiles)
                for t in tiles:
                    last = nc.vector.bn_stats(stats[:, b, t, :], src(t))
                link(last)
                for t in tiles:
                    last = nc.vector.bn_aggr(mean_var[:, b, t, :], stats[:, b, t, :])
                link(last)
                a, z_ = tiles[0], tiles[-1] + 1
                nc.vector.tensor_scalar(var_eps[:, b, a:z_], mean_var[:, b, a:z_, 1], 1.0 if scale is None else scale,
                                        eps, ALU.mult, ALU.add).then_inc(var_ready, 1)
                roots[0] += 1

            def normalise(b, src, dst, ready, factor=rstd, tiles=range(TT)):
                dve.wait_ge(rstd_ready, roots[0])
                for t in tiles:
                    nc.vector.tensor_scalar(dst(t), src(t), mean_var[:, b, t, 0:1], factor[:, b, t:t + 1],
                                            ALU.subtract, ALU.mult).then_inc(ready, 1)

            dve.wait_ge(loaded["x"], 16)
            for b in range(B):
                moments(b, lambda t: x_sb[:, TT * b + t, :])
                normalise(b, lambda t: x_sb[:, TT * b + t, :], lambda t: z[:, TT * b + t, :], z_ready[b])

            dve.wait_ge(loaded["mask"], 16)
            nc.vector.tensor_scalar(mask_bias[:], mask_sb[:], 0.5, MASKED, ALU.is_le, ALU.mult).then_inc(mask_ready, 1)
            dve.wait_ge(loaded["col"], 16)
            nc.vector.tensor_scalar(res2[:, 0:1], col[:, C_RS:C_RS + 1], 0.0, 0.3, ALU.max, ALU.min).then_inc(res_ready, 1)
            dve.wait_ge(res_ready, 1)
            nc.vector.tensor_tensor(res2[:, 1:2], res2[:, 0:1], res2[:, 0:1], ALU.mult).then_inc(res_ready, 1)

            def first_attention(b):
                for t in range(TT):
                    dve.wait_ge(*filled("kv", b, t))
                    if b > 0 and t == 0:
                        dve.wait_ge(norms_ready[b - 1], 2 * TT)
                    nc.vector.tensor_tensor(kv[:, t].rearrange("p a d -> p (a d)"), ps[:, bank("kv", b, t), :],
                                            row[:, R_BKV:R_BKV + 2 * D], ALU.add).then_inc(*take("kv", b, t))
                dve.wait_ge(*taken("kv", b, 0))
                dve.wait_ge(*taken("kv", b, 1))
                for t in range(TT):
                    nc.vector.tensor_tensor(turned[:, t], kv[:, t, :, 0:ROT],
                                            cos[:, t].unsqueeze(1).to_broadcast([P, 2, ROT]), ALU.mult)
                nc.vector.tensor_tensor(kv_prod[:, b, :, ROT:], kv[:, :, 0, ROT:], kv[:, :, 1, ROT:], ALU.mult).then_inc(prod_ready[b], 1)
                dve.wait_ge(prod_ready[b], 1)
                dve.wait_ge(crossed_ready[b], 1)
                link(nc.vector.tensor_tensor(turned[:], turned[:], crossed[:], ALU.add))
                nc.vector.tensor_tensor(kv_prod[:, b, :, 0:ROT], turned[:, :, 0, :], turned[:, :, 1, :], ALU.mult).then_inc(prod_ready[b], 1)

            def gate_queries(b):
                dve.wait_ge(*filled("a", b))
                nc.vector.tensor_scalar(gate_a[:, b, :], ps[:, bank("a", b), 0:DC], 0.5, 0.5,
                                        ALU.mult, ALU.add).then_inc(*take("a", b))
                dve.wait_ge(*taken("a", b))
                dve.wait_ge(*filled("aq", b))
                for c in range(DC):
                    last = nc.vector.tensor_scalar(aq_t[:, c, S * b:S * (b + 1)], ps[:, bank("aq", b), S * c:S * (c + 1)],
                                            col[:, C_BIN + c:C_BIN + c + 1], gate_a[:, b, c:c + 1],
                                            ALU.add, ALU.mult)
                last.then_inc(*take("aq", b))

            def v_bias(b, n):
                dve.wait_ge(*filled("v", b, n))
                dve.wait_ge(v_ones, b + 1)
                for i in range(2):
                    kt = b * KT + 2 * n + i
                    last = nc.vector.tensor_tensor(v_sb[:, kt, :, 0:HD],
                                            ps[:, bank("v", b, n), D * i:D * (i + 1)].rearrange("p (h d) -> p h d", d=HD),
                                            row[:, R_BV:R_BV + D].rearrange("p (h d) -> p h d", d=HD), ALU.add)
                last.then_inc(*take("v", b, n))

            def stream1(b):
                dve.wait_ge(*filled("y", b))
                dve.wait_ge(x2b_ready, b + 1)
                nc.vector.tensor_tensor(h1[:], ps[:, bank("y", b), :].rearrange("p (t d) -> p t d", t=TT),
                                        x2b[:, TT * b:TT * (b + 1)], ALU.add).then_inc(*take("y", b))
                dve.wait_ge(*taken("y", b))
                moments(b, lambda t: h1[:, t, :])
                normalise(b, lambda t: h1[:, t, :], lambda t: x1[:, TT * b + t, :], x1_ready[b])

            def split_q(b):
                dve.wait_ge(*taken("q", b))
                if b > 0:
                    dve.wait_ge(q_stored[b - 1][0], 16)
                nc.vector.tensor_copy(q_part[0][:], q_f[:]).then_inc(qpart_ready[b], 1)
                dve.wait_ge(qpart_ready[b], 1)
                link(nc.vector.tensor_tensor(q_rest[:], q_f[:], q_part[0][:], ALU.subtract))
                if b > 0:
                    dve.wait_ge(q_stored[b - 1][1], 16)
                nc.vector.tensor_copy(q_part[1][:], q_rest[:]).then_inc(qpart_ready[b], 1)
                dve.wait_ge(qpart_ready[b], 2)
                if b > 0:
                    dve.wait_ge(q_stored[b - 1][2], 16)
                nc.vector.tensor_tensor(q_part[2][:], q_rest[:], q_part[1][:], ALU.subtract).then_inc(qpart_ready[b], 1)

            dve.wait_ge(loaded["row"], 16)
            dve.wait_ge(loaded["cos"], 16)
            first_attention(0)
            first_attention(1)
            gate_queries(0)
            stream1(0)
            v_bias(0, 0)
            v_bias(0, 1)
            gate_queries(1)
            stream1(1)
            v_bias(1, 0)
            split_q(0)
            v_bias(1, 1)
            split_q(1)

            def take_pv(b, g):
                n = b * NG + g
                dve.wait_ge(*filled("pv", b, g))
                if n >= 2:
                    dve.wait_ge(*filled("pvt", *divmod(n - 2, NG)))
                nc.vector.tensor_copy(pv_sb[:, n % 2, :], ps[:, bank("pv", b, g), 0:S]).then_inc(*take("pv", b, g))

            def normalise_ctx(b, g):
                dve.wait_ge(*filled("pvt", b, g))
                t_view = ps[:, bank("pvt", b, g), 0:TT * P].rearrange("p (t h r) -> p t h r", t=TT, r=32)
                link(nc.vector.reciprocal(total_inv[:], t_view[:, :, :, HD]))
                for t in range(TT):
                    last = nc.vector.tensor_tensor(
                        ctx_out[:, t, g * HG * HD:(g + 1) * HG * HD].rearrange("p (h d) -> p h d", d=HD),
                        t_view[:, t, :, 0:HD], total_inv[:, t].unsqueeze(2).to_broadcast([P, HG, HD]), ALU.mult)
                last.then_inc(*take("pvt", b, g))

            def take_ctx(b, c):
                dve.wait_ge(*filled("ctxt", b, c))
                if b > 0:
                    dve.wait_ge(*filled("delta", b - 1))
                nc.vector.tensor_copy(ctx_out_t[:, c, :], ps[:, bank("ctxt", b, c), 0:S]).then_inc(*take("ctxt", b, c))

            def stream2_norm(b):
                dve.wait_ge(*filled("delta", b))
                nc.vector.tensor_tensor(delta, ps[:, bank("delta", b), :].rearrange("p (t d) -> p t d", t=TT),
                                        row_of(R_BO), ALU.add).then_inc(*take("delta", b))
                dve.wait_ge(*taken("delta", b))
                moments(b, lambda t: delta[:, t, :], scale=res2[:, 1:2])

            def stream2_sum(b):
                dve.wait_ge(rstd_ready, roots[0])
                for t in range(TT):
                    last = nc.vector.tensor_scalar(delta[:, t, :], delta[:, t, :], mean_var[:, b, t, 0:1], rstd_rs[:, b, t:t + 1],
                                                   ALU.subtract, ALU.mult)
                link(last)
                link(nc.vector.tensor_tensor(delta, delta, row_of(R_LG), ALU.mult))
                dve.wait_ge(x1b_ready[b], 1)
                link(nc.vector.tensor_tensor(delta, delta, x1b[:, TT * b:TT * (b + 1)], ALU.add))
                moments(b, lambda t: delta[:, t, :])

            def stream2(b):
                normalise(b, lambda t: delta[:, t, :], lambda t: x2[:, TT * b + t, :], x2_ready[b])

            dve.wait_ge(res_ready, 2)
            for b in range(B):
                for s in range(STEPS):
                    e = exp_of(b, s)
                    dve.wait_ge(*taken("scores", b, s))
                    w = weights[:, (e - 1) % NE].rearrange("p h s -> p (h s)")
                    nc.vector.tensor_scalar(w, w, E_HIGH, E_LOW, ALU.min, ALU.max).then_inc(clipped, 1)
                    g = s // KT - 1
                    if s % KT == 0:
                        if g >= 0:
                            take_pv(b, g)
                        elif b > 0:
                            take_pv(b - 1, NG - 1)
                    if g >= 0 and s % KT == 2:
                        normalise_ctx(b, g)
                    if b == 1 and s == 3:
                        normalise_ctx(0, NG - 1)
                    if b == 1 and s == 5:
                        take_ctx(0, 1)
                    if b == 1 and s == 7:
                        stream2_norm(0)
                    if b == 1 and s == 9:
                        stream2_sum(0)
                    if b == 1 and s == 11:
                        stream2(0)
                    if s % KT == 0 and g == 2:
                        take_ctx(b, 0)
            take_pv(1, NG - 1)
            normalise_ctx(1, NG - 1)

            pair = [0]

            def gated(b, m):
                dve.wait_ge(*filled("up", b, m))
                pair[0] += 1
                dve.wait_ge(*taken("gate", b, m))
                if b > 0:
                    dve.wait_ge(*filled("down", b - 1, TT - 1))
                for i in range(2):
                    last = nc.vector.scalar_tensor_tensor(out=hidden[:, 2 * m + i, :], in0=ps[:, bank("up", b, m), S * i:S * (i + 1)],
                                                   scalar=col[:, C_US + 2 * m + i:C_US + 2 * m + i + 1],
                                                   in1=silu[:, (pair[0] - 1) % 2, i, :], op0=ALU.mult,
                                                   op1=ALU.mult)
                last.then_inc(*take("up", b, m))

            def output(b, tiles):
                tiles = list(tiles)
                dve.wait_ge(*((x2_ready[B - 1], TT) if b == 0 else (final_ready, TT * b)))
                for t in tiles:
                    dve.wait_ge(*filled("down", b, t))
                    nc.vector.tensor_tensor(delta[:, t, :], ps[:, bank("down", b, t), 0:D], row[:, R_DS:R_DS + D],
                                            ALU.mult).then_inc(*take("down", b, t))
                dve.wait_ge(*taken("down", b, tiles[-1]))
                for t in tiles:
                    last = nc.vector.tensor_tensor(delta[:, t, :], delta[:, t, :], x2[:, TT * b + t, :], ALU.add)
                link(last)
                moments(b, lambda t: delta[:, t, :], tiles=tiles)
                normalise(b, lambda t: delta[:, t, :], lambda t: final[:, TT * b + t, :], final_ready, tiles=tiles)

            gated(0, 0)
            take_ctx(1, 1)
            stream2_norm(1)
            gated(0, 1)
            stream2_sum(1)
            gated(0, 2)
            stream2(1)
            output(0, range(TT))
            for m in range(FC // 2):
                gated(1, m)
            for t in range(TT):
                output(1, [t])

        @block.tensor
        def _(pe):
            done = []

            def begin(*job):
                assert ORDER[len(done)] == job, (ORDER[len(done)], job)
                done.append(job)
                for earlier in PLAN.before[job]:
                    pe.wait_ge(*taken(*earlier))

            def transposes(job, src, ready, need):
                begin(*job)
                pe.wait_ge(ready, need)
                for c in range(DC):
                    for t in range(TT):
                        last = nc.tensor.transpose(ps[:, bank(*job), S * c + P * t:S * c + P * (t + 1)],
                                                   src[:, TT * job[1] + t, P * c:P * (c + 1)], ident[:])
                last.then_inc(*full(*job))

            def k_proj(b, c):
                begin("k", b, c)
                for i in range(DC):
                    last = nc.tensor.matmul(ps[:, bank("k", b, c), :], wk_sb[:, i, P * c:P * (c + 1)],
                                            ctx_sb[:, i, T * b:T * (b + 1)], start=(i == 0), stop=(i == DC - 1))
                last.then_inc(*full("k", b, c))

            def kv_proj(b, t):
                begin("kv", b, t)
                n = TT * b + t
                for i in range(DC):
                    last = nc.tensor.matmul(ps[:, bank("kv", b, t), :], z_t[:, i, P * n:P * (n + 1)],
                                            w_in_sb[:, i, D:3 * D], start=(i == 0), stop=(i == DC - 1))
                last.then_inc(*full("kv", b, t))

            def feature_proj(job, w, src):
                b = job[1]
                begin(*job)
                for c in range(DC):
                    for i in range(DC):
                        last = nc.tensor.matmul(ps[:, bank(*job), S * c:S * (c + 1)], w[:, i, P * c:P * (c + 1)],
                                                src[:, i, S * b:S * (b + 1)], start=(i == 0), stop=(i == DC - 1))
                last.then_inc(*full(*job))

            def token_proj(job, w, src, offset):
                begin(*job)
                for t in range(TT):
                    for i in range(DC):
                        last = nc.tensor.matmul(ps[:, bank(*job), D * t:D * (t + 1)],
                                                src[:, i, offset + P * t:offset + P * (t + 1)], w[:, i, :],
                                                start=(i == 0), stop=(i == DC - 1))
                last.then_inc(*full(*job))

            def similarity(b):
                begin("a", b)
                pe.wait_ge(prod_ready[b], 2)
                pe.wait_ge(pair_ready[b], 1)
                for c in range(DC):
                    for t in range(TT):
                        last = nc.tensor.matmul(ps[:, bank("a", b), c:c + 1], kv_prod[:, b, t, P * c:P * (c + 1)],
                                                pair_inv[:, b, t:t + 1], start=(t == 0), stop=(t == TT - 1))
                last.then_inc(*full("a", b))

            def y_proj(b):
                pe.wait_ge(*taken("aq", b))
                token_proj(("y", b), w_out_sb, aq_t, S * b)

            def q_proj(b):
                pe.wait_ge(*taken("x1t", b))
                feature_proj(("q", b), wq_sb, x1_t)

            pe.wait_ge(loaded["wk"], 16)
            pe.wait_ge(loaded["ctx0"], 16)
            k_proj(0, 0)
            k_proj(0, 1)
            pe.wait_ge(ident_ready, 1)
            transposes(("zt", 0), z, z_ready[0], 2)
            transposes(("zt", 1), z, z_ready[1], 2)
            pe.wait_ge(loaded["w_in"], 16)
            for b in range(B):
                pe.wait_ge(*taken("zt", b))
                kv_proj(b, 0)
                kv_proj(b, 1)
                feature_proj(("aq", b), w_in_sb, z_t)
            pe.wait_ge(loaded["ctx1"], 16)
            k_proj(1, 0)
            similarity(0)
            k_proj(1, 1)
            pe.wait_ge(loaded["w_out"], 16)
            y_proj(0)
            pe.wait_ge(loaded["wv"], 16)
            token_proj(("v", 0, 0), wv_sb, ctx_sb, 0)
            token_proj(("v", 0, 1), wv_sb, ctx_sb, S)
            similarity(1)
            y_proj(1)
            transposes(("x1t", 0), x1, x1_ready[0], 2)
            token_proj(("v", 1, 0), wv_sb, ctx_sb, T)
            pe.wait_ge(loaded["wq"], 16)
            q_proj(0)
            token_proj(("v", 1, 1), wv_sb, ctx_sb, T + S)
            transposes(("x1t", 1), x1, x1_ready[1], 2)
            q_proj(1)

            def scores(b, s):
                g, kt = divmod(s, KT)
                begin("scores", b, s)
                k0 = bank("scores", b, s)
                for j in range(HG):
                    h = g * HG + j
                    last = nc.tensor.matmul(ps[:, k0 + j // 2, S * (j % 2):S * (j % 2 + 1)],
                                            k_stack[:, h, T * b + P * kt:T * b + P * (kt + 1)],
                                            q_stack[:, h, S * b:S * (b + 1)], start=True, stop=True)
                last.then_inc(*full("scores", b, s))

            def weigh(b, s):
                g, kt = divmod(s, KT)
                e = exp_of(b, s)
                if kt == 0:
                    begin("pv", b, g)
                pe.wait_ge(clipped, e)
                for j in range(HG):
                    last = nc.tensor.matmul(ps[32 * j:32 * (j + 1), bank("pv", b, g), 0:S],
                                            v_sb[:, b * KT + kt, g * HG + j, :], weights[:, (e - 1) % NE, j, :],
                                            start=(kt == 0), stop=(kt == KT - 1))
                last.then_inc(*(full("pv", b, g) if kt == KT - 1 else (weights_used, 1)))

            def transpose_pv(b, g):
                n = b * NG + g
                begin("pvt", b, g)
                pe.wait_ge(*taken("pv", b, g))
                for t in range(TT):
                    last = nc.tensor.transpose(ps[:, bank("pvt", b, g), P * t:P * (t + 1)],
                                               pv_sb[:, n % 2, P * t:P * (t + 1)], ident[:])
                last.then_inc(*full("pvt", b, g))

            def transpose_ctx(b, c):
                begin("ctxt", b, c)
                pe.wait_ge(*taken("pvt", b, 2 * c))
                pe.wait_ge(*taken("pvt", b, 2 * c + 1))
                for t in range(TT):
                    last = nc.tensor.transpose(ps[:, bank("ctxt", b, c), P * t:P * (t + 1)],
                                               ctx_out[:, t, P * c:P * (c + 1)], ident[:])
                last.then_inc(*full("ctxt", b, c))

            def out_proj(b):
                pe.wait_ge(*taken("ctxt", b, 0))
                pe.wait_ge(*taken("ctxt", b, 1))
                token_proj(("delta", b), wo_sb, ctx_out_t, 0)

            pe.wait_ge(loaded["wo"], 16)
            for b in range(B):
                pe.wait_ge(k_stacked[b], 16 * len(K_PARTS))
                pe.wait_ge(q_stacked[b], 16 * len(Q_PARTS))
                pe.wait_ge(*taken("v", b, 0))
                pe.wait_ge(*taken("v", b, 1))
                scores(b, 0)
                scores(b, 1)
                for s in range(STEPS):
                    if s + 2 < STEPS:
                        scores(b, s + 2)
                    weigh(b, s)
                    g = s // KT - 1
                    if g >= 0 and s % KT == 1:
                        transpose_pv(b, g)
                    if g >= 0 and s % KT == 3 and g % 2 == 1:
                        transpose_ctx(b, g // 2)
                    if b == 1 and s == 2:
                        transpose_pv(0, NG - 1)
                    if b == 1 and s == 4:
                        transpose_ctx(0, 1)
                    if b == 1 and s == 6:
                        out_proj(0)
                    if b == 1 and s == 14:
                        transposes(("x2t", 0), x2, x2_ready[0], 2)
            transpose_pv(1, NG - 1)

            def inner(kind, w, b, m):
                begin(kind, b, m)
                for i in range(2):
                    f = 2 * m + i
                    for c in range(DC):
                        last = nc.tensor.matmul(ps[:, bank(kind, b, m), S * i:S * (i + 1)], w[:, c, P * f:P * (f + 1)],
                                                x2_t[:, c, S * b:S * (b + 1)], start=(c == 0), stop=(c == DC - 1))
                last.then_inc(*full(kind, b, m))

            def down(b, t):
                begin("down", b, t)
                for f in range(FC):
                    pe.wait_ge(*taken("up", b, f // 2))
                    last = nc.tensor.matmul(ps[:, bank("down", b, t), 0:D], hidden[:, f, P * t:P * (t + 1)],
                                            down_sb[:, f, :], start=(f == 0), stop=(f == FC - 1))
                last.then_inc(*full("down", b, t))

            pe.wait_ge(loaded["gate"], 16)
            pe.wait_ge(loaded["up"], 16)
            pe.wait_ge(*taken("x2t", 0))
            inner("gate", gate_sb, 0, 0)
            inner("up", up_sb, 0, 0)
            transpose_ctx(1, 1)
            inner("gate", gate_sb, 0, 1)
            out_proj(1)
            inner("up", up_sb, 0, 1)
            inner("gate", gate_sb, 0, 2)
            inner("up", up_sb, 0, 2)
            pe.wait_ge(loaded["down"], 16)
            down(0, 0)
            down(0, 1)
            transposes(("x2t", 1), x2, x2_ready[1], 2)
            pe.wait_ge(*taken("x2t", 1))
            for m in range(FC // 2):
                inner("gate", gate_sb, 1, m)
                inner("up", up_sb, 1, m)
            down(1, 0)
            down(1, 1)


def kernel(x, ctx_2048, mask_BxS2_ik0, L0_attn_W_in, L0_attn_b_in, L0_attn_W_out, L0_attn_b_out,
           L0_attn_gamma, L0_attn_beta, L0_xattn_Wq, L0_xattn_bq, L0_xattn_Wk, L0_xattn_bk, L0_xattn_Wv,
           L0_xattn_bv, L0_xattn_Wo, L0_xattn_bo, L0_xattn_ln_gamma, L0_xattn_ln_beta,
           L0_xattn_residual_scale, L0_ffn_gate_w, L0_ffn_up_w, L0_ffn_down_w, L0_ffn_gate_s,
           L0_ffn_up_s, L0_ffn_down_s):
    import concourse.bacc as bacc
    from concourse.bass_utils import run_bass_kernel_spmd

    f32 = np.float32

    def chunked(a):
        return np.asarray(a).reshape(-1, P).T

    def padded(a):
        a = np.asarray(a)
        return np.concatenate([a, np.zeros((FC * P - a.shape[0],) + a.shape[1:], a.dtype)])

    cols = np.concatenate([chunked(L0_attn_gamma), chunked(L0_attn_beta), chunked(np.asarray(L0_attn_b_in)[:D]),
                           chunked(L0_xattn_bq), chunked(L0_xattn_bk), chunked(padded(L0_ffn_gate_s)),
                           chunked(padded(L0_ffn_up_s)),
                           np.broadcast_to(np.asarray(L0_xattn_residual_scale), (P, 1))], axis=1)
    rows = np.concatenate([np.asarray(a) for a in (
        np.asarray(L0_attn_b_in)[D:], L0_attn_b_out, L0_xattn_bv, L0_xattn_bo, L0_xattn_ln_gamma,
        L0_xattn_ln_beta, L0_ffn_down_s)])[None]
    inv_freq = f32(1.0) / f32(10000.0) ** (np.arange(0, ROT, 2, dtype=f32) / f32(ROT))
    angle = np.repeat(np.arange(S, dtype=f32)[:, None] * inv_freq[None, :], 2, axis=1)
    sign = np.tile(np.array([-1.0, 1.0], f32), ROT // 2)
    arrays = {
        "x": np.asarray(x).reshape(B * S, D),
        "ctx_t": np.asarray(ctx_2048).reshape(B * T, D).T,
        "mask_cols": np.asarray(mask_BxS2_ik0).reshape(B * KT, P).T,
        "cols": cols,
        "rows": rows,
        "rope_cos": np.cos(angle).astype(f32),
        "rope_sin": (np.sin(angle) * sign).astype(f32),
        "w_in": np.asarray(L0_attn_W_in),
        "w_out": np.asarray(L0_attn_W_out),
        "wq_t": np.asarray(L0_xattn_Wq).T,
        "wk_t": np.asarray(L0_xattn_Wk).T,
        "wv_t": np.asarray(L0_xattn_Wv).T,
        "wo_t": np.asarray(L0_xattn_Wo).T,
        "gate_t": padded(L0_ffn_gate_w).T,
        "up_t": padded(L0_ffn_up_w).T,
        "down_t": padded(np.asarray(L0_ffn_down_w).T),
    }
    arrays = {name: np.ascontiguousarray(a) for name, a in arrays.items()}

    nc = bacc.Bacc("TRN2", target_bir_lowering=False, num_devices=1)
    args = [nc.dram_tensor(name, a.shape, mybir.dt.from_np(a.dtype), kind="ExternalInput").ap()
            for name, a in arrays.items()]
    out = nc.dram_tensor("out", (B * S, D), F32, kind="ExternalOutput").ap()
    decoder_layer(nc, *args, out)
    result = run_bass_kernel_spmd(nc, [arrays], core_ids=[0])
    return result.results[0]["out"].reshape(B, S, D)
```

```python
from contextlib import ExitStack

import numpy as np

import concourse.bass as bass
from concourse import mybir

ALU = mybir.AluOpType
ACT = mybir.ActivationFunctionType
F32 = mybir.dt.float32
BF16 = mybir.dt.bfloat16
I32 = mybir.dt.int32

P = 128
B = 2
S = 256
T = 512
D = 256
ROT = D // 2
DC = D // P
TT = S // P
KT = T // P
NH = 16
HD = D // NH
HG = 4
NG = NH // HG
FC = 6
EPS = 1e-5
SCORE_SCALE = 1.0 / np.sqrt(HD)
E_LOW = float(np.exp(np.float32(-50.0)))
E_HIGH = float(np.exp(np.float32(50.0)))
MASKED = -3.0e38
STEPS = NG * KT
NE = 4
Q_PARTS = (0, 1, 2, 0, 1, 2, 0, 1)
K_PARTS = (0, 0, 0, 1, 1, 1, 2, 2)

C_GAMMA, C_BETA, C_BIN, C_BQ, C_BK, C_GS, C_US, C_RS = 0, 2, 4, 6, 8, 10, 16, 22
NCOL = 23
R_BKV, R_BOUT, R_BV, R_BO, R_LG, R_LB, R_DS = 0, 512, 768, 1024, 1280, 1536, 1792
NROW = 2048


WARM_UP = 26


class Plan:

    def __init__(self, jobs):
        self.at = {}
        self.before = {}
        count = [0] * 8
        last = {}
        for name, banks in jobs:
            count[banks[0]] += 1
            self.at[name] = (banks, count[banks[0]])
            self.before[name] = []
            for k in banks:
                if k in last and last[k] not in self.before[name]:
                    self.before[name].append(last[k])
                last[k] = name


def after_weigh(b, s):
    jobs = []
    g = s // KT - 1
    if s % KT == 1 and g >= 0:
        jobs.append(("pvt", b, g))
    if s % KT == 3 and g == 1:
        jobs.append(("ctxt", b, 0))
    if b > 0:
        jobs += {1: [("pvt", b - 1, NG - 1)], 3: [("ctxt", b - 1, 1)], 5: [("delta", b - 1)],
                 13: [("x2t", b - 1)]}.get(s, [])
    return jobs


def plan():
    jobs = [
        (("zt", 0), [0]), (("kv", 0, 0), [1]), (("kv", 0, 1), [2]), (("zt", 1), [3]), (("aq", 0), [4]),
        (("kv", 1, 0), [5]), (("kv", 1, 1), [6]), (("a", 0), [0]), (("aq", 1), [7]), (("y", 0), [1]),
        (("k", 0, 0), [2]), (("a", 1), [3]), (("k", 0, 1), [0]), (("x1t", 0), [5]), (("y", 1), [6]),
        (("q", 0), [4]), (("v", 0, 0), [7]), (("v", 0, 1), [1]), (("k", 1, 0), [2]), (("x1t", 1), [3]),
        (("k", 1, 1), [0]), (("q", 1), [5]), (("v", 1, 0), [6]),
    ]
    steps = [(b, s) for b in range(B) for s in range(STEPS)]
    jobs += [(("scores",) + steps[n], [2 * (n % 2), 2 * (n % 2) + 1]) for n in range(2)]
    jobs += [(("v", 1, 1), [7])]
    for n, (b, s) in enumerate(steps):
        if n + 2 < len(steps):
            jobs.append((("scores",) + steps[n + 2], [2 * (n % 2), 2 * (n % 2) + 1]))
        g = s // KT
        if s % KT == 0:
            jobs.append((("pv", b, g), [4 + g % 2]))
        for job in after_weigh(b, s):
            jobs.append((job, [7 if job[0] in ("delta", "x2t") else 6 + job[-1] % 2 if job[0] == "pvt" else 7]))
    jobs += [(("pvt", 1, NG - 1), [6]), (("gate", 0, 0), [0]), (("ctxt", 1, 1), [7]), (("up", 0, 0), [2]),
             (("delta", 1), [6]), (("gate", 0, 1), [1]), (("up", 0, 1), [3]),
             (("gate", 0, 2), [0]), (("up", 0, 2), [2]), (("down", 0, 0), [4]), (("x2t", 1), [7]),
             (("down", 0, 1), [5]),
             (("gate", 1, 0), [1]), (("up", 1, 0), [3]), (("gate", 1, 1), [0]), (("up", 1, 1), [2]),
             (("gate", 1, 2), [1]), (("up", 1, 2), [3]), (("down", 1, 0), [6]), (("down", 1, 1), [7])]
    return Plan(jobs), [name for name, _ in jobs]


PLAN, ORDER = plan()


def decoder_layer(nc, x, ctx_t, mask_cols, cols, rows, rope_cos, rope_sin, w_in, w_out,
                  wq_t, wk_t, wv_t, wo_t, gate_t, up_t, down_t, out):
    with ExitStack() as stack:
        def sb(name, shape, dt=F32):
            return stack.enter_context(nc.sbuf_tensor(name, shape, dt))

        def sem(name):
            return stack.enter_context(nc.semaphore(name))

        def per_batch(name):
            return [sem(f"{name}{b}") for b in range(B)]

        w_in_sb = sb("w_in_sb", [P, DC, 3 * D])
        w_out_sb = sb("w_out_sb", [P, DC, D])
        wq_sb = sb("wq_sb", [P, DC, D])
        wk_sb = sb("wk_sb", [P, DC, D])
        wv_sb = sb("wv_sb", [P, DC, D])
        wo_sb = sb("wo_sb", [P, DC, D])
        gate_sb = sb("gate_sb", [P, DC, FC * P])
        up_sb = sb("up_sb", [P, DC, FC * P])
        down_sb = sb("down_sb", [P, FC, D])
        col = sb("col", [P, NCOL])
        row = sb("row", [P, NROW])
        cos = sb("cos", [P, TT, ROT])
        sin = sb("sin", [P, TT, ROT])
        mask_sb = sb("mask_sb", [P, B * KT], I32)
        mask_bias = sb("mask_bias", [P, B * KT])
        ident = sb("ident", [P, P])
        power = sb("power", [P, 4])
        res2 = sb("res2", [P, 2])
        x_sb = sb("x_sb", [P, B * TT, D])
        x2b = sb("x2b", [P, B * TT, D])
        stats = sb("stats", [P, B, TT, 6])
        mean_var = sb("mean_var", [P, B, TT, 2])
        var_eps = sb("var_eps", [P, B, TT])
        rstd = sb("rstd", [P, B, TT])
        rstd_rs = sb("rstd_rs", [P, B, TT])
        z = sb("z", [P, B * TT, D])
        z_t = sb("z_t", [P, DC, B * S])
        kv = sb("kv", [P, TT, 2, D])
        turned = sb("turned", [P, TT, 2, ROT])
        crossed = sb("crossed", [P, TT, 2, ROT])
        kv_prod = sb("kv_prod", [P, B, TT, D])
        squares = sb("squares", [P, TT, 2, D], BF16)
        norm_sq = sb("norm_sq", [P, B, TT, 2])
        norm_inv = sb("norm_inv", [P, B, TT, 2])
        pair_inv = sb("pair_inv", [P, B, TT])
        gate_a = sb("gate_a", [P, B, DC])
        aq_t = sb("aq_t", [P, DC, B * S])
        x1 = sb("x1", [P, B * TT, D])
        x1b = sb("x1b", [P, B * TT, D])
        x1_t = sb("x1_t", [P, DC, B * S])
        ctx_sb = sb("ctx_sb", [P, DC, B * T])
        k_rest = sb("k_rest", [P, DC, T])
        k_part = [sb(f"k_part{i}", [P, DC, T], BF16) for i in range(3)]
        q_rest = sb("q_rest", [P, DC, S])
        q_part = [sb(f"q_part{i}", [P, DC, S], BF16) for i in range(3)]
        k_stack = sb("k_stack", [P, B, NH, T], BF16)
        q_stack = sb("q_stack", [P, B, NH, S], BF16)
        v_sb = sb("v_sb", [P, B * KT, NH, 32])
        weights = sb("weights", [P, NE, HG, S])
        pv_sb = sb("pv_sb", [P, 2, S])
        total_inv = sb("total_inv", [P, TT, HG])
        ctx_out_t = sb("ctx_out_t", [P, DC, S])
        ctx_out = crossed[:].rearrange("p t a r -> p t (a r)")
        delta = turned[:].rearrange("p t a r -> p t (a r)")
        x2 = x2b[:]
        x2_t = z_t[:]
        silu = k_rest[:].rearrange("p c (a s) -> p c a s", a=2)
        hidden = ctx_sb[:].rearrange("p c (f s) -> p (c f) s", s=S)[:, 0:FC]
        final = z[:]

        ps = stack.enter_context(nc.psum_tensor("ps", [P, 8, 512], F32))
        q_scratch = nc.dram_tensor("q_scratch", (B, 3, HD, NH, S), BF16, kind="Internal").ap()
        k_scratch = nc.dram_tensor("k_scratch", (B, 3, HD, NH, T), BF16, kind="Internal").ap()

        loaded = {n: sem(f"loaded_{n}") for n in
                  ("x0", "x1", "col", "row", "late_row", "cos", "sin", "mask", "ctx0", "ctx1", "wk", "wv", "w_kv", "w_q", "w_out",
                   "wq", "wo", "gate", "up", "down")}
        bank_filled = [sem(f"bank_filled{k}") for k in range(8)]
        bank_taken = [sem(f"bank_taken{k}") for k in range(8)]
        const_ready = sem("const_ready")
        ident_ready = sem("ident_ready")
        mask_ready = sem("mask_ready")
        res_ready = sem("res_ready")
        v_ones = sem("v_ones")
        var_ready = sem("var_ready")
        rstd_ready = sem("rstd_ready")
        dve_step = sem("dve_step")
        pool_step = sem("pool_step")
        z_ready = per_batch("z_ready")
        crossed_ready = per_batch("crossed_ready")
        prod_ready = per_batch("prod_ready")
        norms_ready, pair_ready = per_batch("norms_ready"), per_batch("pair_ready")
        x1_ready, x1b_ready, x2_ready = per_batch("x1_ready"), per_batch("x1b_ready"), per_batch("x2_ready")
        k1_ready, krest_ready = per_batch("k1_ready"), per_batch("krest_ready")
        k2_ready, k3_ready = per_batch("k2_ready"), per_batch("k3_ready")
        q1_ready, qrest_ready = per_batch("q1_ready"), per_batch("qrest_ready")
        q2_ready, q3_ready = per_batch("q2_ready"), per_batch("q3_ready")
        k_stored = [[sem(f"k_stored{b}{i}") for i in range(3)] for b in range(B)]
        q_stored = [[sem(f"q_stored{b}{i}") for i in range(3)] for b in range(B)]
        k_stacked = per_batch("k_stacked")
        q_stacked_first, q_stacked_rest = per_batch("q_stacked_first"), per_batch("q_stacked_rest")
        clipped = sem("clipped")
        weights_used = sem("weights_used")
        down_scaled = sem("down_scaled")
        final_ready = sem("final_ready")
        stored = sem("stored")

        def filled(*job):
            banks, n = PLAN.at[job]
            return bank_filled[banks[0]], n

        def taken(*job):
            banks, n = PLAN.at[job]
            return bank_taken[banks[0]], n

        def bank(*job):
            return PLAN.at[job][0][0]

        def full(*job):
            return bank_filled[bank(*job)], 1

        def take(*job):
            return bank_taken[bank(*job)], 1

        def used(n):
            if n % KT == KT - 1:
                return filled("pv", *divmod(n // KT, NG))
            return weights_used, n - n // KT + 1

        def exp_of(b, s):
            return b * STEPS + s + 1

        block = stack.enter_context(nc.Block())

        @block.sync
        def _(sp):
            def by_chunk(a):
                return a.rearrange("(c p) n -> p c n", p=P)

            def batch(b, n):
                return slice(n * b, n * (b + 1))

            x_v = x.rearrange("(t p) d -> p t d", p=P)
            sp.dma_start(x_sb[:, batch(0, TT)], x_v[:, batch(0, TT)]).then_inc(loaded["x0"], 16)
            sp.dma_start(w_in_sb[:, :, D:], by_chunk(w_in)[:, :, D:]).then_inc(loaded["w_kv"], 16)
            sp.dma_start(x_sb[:, batch(1, TT)], x_v[:, batch(1, TT)]).then_inc(loaded["x1"], 16)
            sp.dma_start(row[:, 0:R_BV], rows[:, 0:R_BV].to_broadcast([P, R_BV])).then_inc(loaded["row"], 16)
            sp.dma_start(cos[:], rope_cos.rearrange("(t p) d -> p t d", p=P)).then_inc(loaded["cos"], 16)
            sp.dma_start(sin[:], rope_sin.rearrange("(t p) d -> p t d", p=P)).then_inc(loaded["sin"], 16)
            sp.dma_start(w_in_sb[:, :, 0:D], by_chunk(w_in)[:, :, 0:D]).then_inc(loaded["w_q"], 16)
            sp.dma_start(w_out_sb[:], by_chunk(w_out)).then_inc(loaded["w_out"], 16)
            sp.dma_start(wk_sb[:], by_chunk(wk_t)).then_inc(loaded["wk"], 16)
            sp.dma_start(ctx_sb[:, :, batch(0, T)], by_chunk(ctx_t)[:, :, batch(0, T)]).then_inc(loaded["ctx0"], 16)
            sp.dma_start(wq_sb[:], by_chunk(wq_t)).then_inc(loaded["wq"], 16)
            sp.dma_start(wv_sb[:], by_chunk(wv_t)).then_inc(loaded["wv"], 16)
            sp.dma_start(row[:, R_BV:], rows[:, R_BV:].to_broadcast([P, NROW - R_BV])).then_inc(loaded["late_row"], 16)
            sp.dma_start(ctx_sb[:, :, batch(1, T)], by_chunk(ctx_t)[:, :, batch(1, T)]).then_inc(loaded["ctx1"], 16)
            sp.dma_start(wo_sb[:], by_chunk(wo_t)).then_inc(loaded["wo"], 16)
            sp.dma_start(gate_sb[:], by_chunk(gate_t)).then_inc(loaded["gate"], 16)
            sp.dma_start(up_sb[:], by_chunk(up_t)).then_inc(loaded["up"], 16)
            sp.dma_start(down_sb[:], by_chunk(down_t)).then_inc(loaded["down"], 16)

            def store_part(scratch, part, i, b, stored_):
                sp.dma_start(scratch[b, i].rearrange("d (h c) t -> h d (c t)", c=DC),
                             part[i][:].rearrange("p c t -> p (c t)")).then_inc(stored_[b][i], 16)

            def store_k(b, i):
                sp.wait_ge([k1_ready, k2_ready, k3_ready][i][b], DC)
                store_part(k_scratch, k_part, i, b, k_stored)

            def store_q(b, i):
                sp.wait_ge([q1_ready, q2_ready, q3_ready][i][b], 1)
                store_part(q_scratch, q_part, i, b, q_stored)

            def stack_k(b, i):
                n, blocks = K_PARTS.index(i), K_PARTS.count(i)
                sp.wait_ge(k_stored[b][i], 16)
                sp.dma_start(k_stack[HD * n:HD * (n + blocks), b].rearrange("p h t -> p (h t)"),
                             k_scratch[b, i].rearrange("d h t -> d (h t)").unsqueeze(0).to_broadcast(
                                 [blocks, HD, NH * T])).then_inc(k_stacked[b], 16)

            def stack_q(b):
                for i in range(3):
                    sp.wait_ge(q_stored[b][i], 16)
                for h, done in ((slice(0, HG), q_stacked_first[b]), (slice(HG, NH), q_stacked_rest[b])):
                    for rows, times, parts in ((slice(0, 6 * HD), 2, 3), (slice(6 * HD, P), 1, 2)):
                        src = q_scratch[b, 0:parts, :, h].rearrange("i d h t -> (i d) (h t)")
                        if times > 1:
                            src = src.unsqueeze(0).to_broadcast([times, parts * HD, (h.stop - h.start) * S])
                        sp.dma_start(q_stack[rows, b, h].rearrange("p h t -> p (h t)"), src).then_inc(done, 16)

            store_k(0, 0)
            store_k(0, 1)
            stack_k(0, 0)
            store_k(0, 2)
            stack_k(0, 1)
            store_q(0, 0)
            store_q(0, 1)
            store_q(0, 2)
            stack_k(0, 2)
            stack_q(0)
            for i in range(3):
                store_k(1, i)
            for i in range(3):
                store_q(1, i)
            for i in range(3):
                stack_k(1, i)
            stack_q(1)
            for n in range(B * TT):
                sp.wait_ge(final_ready, n + 1)
                sp.dma_start(out[n * P:(n + 1) * P, :], final[:, n, :]).then_inc(stored, 16)
            sp.wait_ge(stored, 16 * B * TT)

        @block.gpsimd
        def _(pool):
            steps = [0]

            def link(ins):
                steps[0] += 1
                ins.then_inc(pool_step, 1)
                pool.wait_ge(pool_step, steps[0])

            nc.gpsimd.memset(power[:], -0.5).then_inc(const_ready, 1)
            link(nc.gpsimd.memset(ident[:], 0.0))
            nc.gpsimd.affine_select(out=ident[:], in_=ident[:], compare_op=ALU.not_equal, fill=1.0, base=0,
                                    pattern=[[-1, P]], channel_multiplier=1).then_inc(ident_ready, 1)
            pool.wait_ge(const_ready, 1)

            uses = [0]

            def inverse_root(b):
                uses[0] += 1
                pool.wait_ge(var_ready, uses[0])
                nc.gpsimd.tensor_tensor(rstd[:, b, :], var_eps[:, b, :], power[:, 0:TT], ALU.pow).then_inc(rstd_ready, 1)

            inverse_root(0)
            inverse_root(1)
            nc.gpsimd.memset(v_sb[:, 0:KT], 1.0).then_inc(v_ones, 1)

            def cross_terms(b):
                pool.wait_ge(loaded["sin"], 16)
                pool.wait_ge(*taken("kv", b, 0))
                pool.wait_ge(*taken("kv", b, 1))
                if b > 0:
                    pool.wait_ge(prod_ready[b - 1], 2)
                for odd in range(2):
                    for t in range(TT):
                        last = nc.gpsimd.tensor_tensor(
                            crossed[:, t, :, odd::2], kv[:, t, :, 1 - odd:ROT:2],
                            sin[:, t, odd::2].unsqueeze(1).to_broadcast([P, 2, ROT // 2]), ALU.mult)
                last.then_inc(crossed_ready[b], 1)

            def norms(b):
                pool.wait_ge(norms_ready[b], 2 * TT)
                link(nc.gpsimd.tensor_tensor(norm_inv[:, b], norm_sq[:, b], power[:, 0:4].rearrange("p (a c) -> p a c", a=2), ALU.pow))
                nc.gpsimd.tensor_tensor(pair_inv[:, b], norm_inv[:, b, :, 0], norm_inv[:, b, :, 1], ALU.mult).then_inc(pair_ready[b], 1)

            cross_terms(0)
            norms(0)
            cross_terms(1)
            norms(1)
            nc.gpsimd.memset(v_sb[:, KT:2 * KT], 1.0).then_inc(v_ones, 1)
            inverse_root(0)
            inverse_root(1)
            pool.wait_ge(loaded["late_row"], 16)
            for b in range(B):
                pool.wait_ge(x1_ready[b], 2)
                nc.gpsimd.tensor_tensor(x1b[:, TT * b:TT * (b + 1)], x1[:, TT * b:TT * (b + 1)],
                                        row[:, R_LB:R_LB + D].unsqueeze(1).to_broadcast([P, TT, D]),
                                        ALU.add).then_inc(x1b_ready[b], 1)
            pool.wait_ge(loaded["down"], 16)
            nc.gpsimd.tensor_tensor(down_sb[:], down_sb[:], row[:, R_DS:R_DS + D].unsqueeze(1).to_broadcast([P, FC, D]),
                                    ALU.mult).then_inc(down_scaled, 1)
            pool.wait_ge(res_ready, 2)

            def after_cross(b):
                uses[0] += 1
                pool.wait_ge(var_ready, uses[0])
                link(nc.gpsimd.tensor_tensor(rstd[:, b, :], var_eps[:, b, :], power[:, 0:TT], ALU.pow))
                nc.gpsimd.tensor_tensor(rstd_rs[:, b, :], rstd[:, b, :],
                                        res2[:, 0:1].to_broadcast([P, TT]), ALU.mult).then_inc(rstd_ready, 1)

            after_cross(0)
            inverse_root(0)
            after_cross(1)
            inverse_root(1)
            inverse_root(0)
            for t in range(TT):
                uses[0] += 1
                pool.wait_ge(var_ready, uses[0])
                nc.gpsimd.tensor_tensor(rstd[:, 1, t:t + 1], var_eps[:, 1, t:t + 1], power[:, 0:1], ALU.pow).then_inc(rstd_ready, 1)

        @block.scalar
        def _(act):
            act.dma_start(col[:], cols).then_inc(loaded["col"], 16)
            act.dma_start(mask_sb[:], mask_cols).then_inc(loaded["mask"], 16)

            def k_first(b, c):
                act.wait_ge(*filled("k", b, c))
                if b > 0:
                    act.wait_ge(k_stored[b - 1][0], 16)
                nc.scalar.activation(k_part[0][:, c, :], ps[:, bank("k", b, c), :], ACT.Identity,
                                     bias=col[:, C_BK + c:C_BK + c + 1]).then_inc(k1_ready[b], 1)

            def k_second(b, c):
                act.wait_ge(*taken("k", b, c))
                if b > 0:
                    act.wait_ge(k_stored[b - 1][1], 16)
                nc.scalar.activation(k_part[1][:, c], k_rest[:, c], ACT.Copy).then_inc(k2_ready[b], 1)

            def q_first(b):
                act.wait_ge(*filled("q", b))
                if b > 0:
                    act.wait_ge(q_stored[b - 1][0], 16)
                for c in range(DC):
                    last = nc.scalar.activation(q_part[0][:, c, :], ps[:, bank("q", b), S * c:S * (c + 1)], ACT.Identity,
                                                bias=col[:, C_BQ + c:C_BQ + c + 1])
                last.then_inc(q1_ready[b], 1)

            def q_second(b):
                act.wait_ge(*taken("q", b))
                if b > 0:
                    act.wait_ge(q_stored[b - 1][1], 16)
                nc.scalar.activation(q_part[1][:], q_rest[:], ACT.Copy).then_inc(q2_ready[b], 1)

            def z_scale(b):
                act.wait_ge(*filled("zt", b))
                for c in range(DC):
                    last = nc.scalar.activation(z_t[:, c, S * b:S * (b + 1)], ps[:, bank("zt", b), S * c:S * (c + 1)],
                                                ACT.Identity, scale=col[:, C_GAMMA + c:C_GAMMA + c + 1],
                                                bias=col[:, C_BETA + c:C_BETA + c + 1])
                last.then_inc(*take("zt", b))

            def square_norms(b, t):
                if b > 0 and t == 0:
                    act.wait_ge(norms_ready[b - 1], 2 * TT)
                act.wait_ge(*taken("kv", b, t))
                for n in range(2):
                    nc.scalar.activation(squares[:, t, n, :], kv[:, t, n, :], ACT.Square,
                                         accum_out=norm_sq[:, b, t, n:n + 1]).then_inc(norms_ready[b], 1)

            def copy_t(job, b, dst):
                act.wait_ge(*filled(job, b))
                nc.scalar.activation(dst[:, :, S * b:S * (b + 1)],
                                     ps[:, bank(job, b), :].rearrange("p (c s) -> p c s", c=DC), ACT.Copy).then_inc(*take(job, b))

            nc.scalar.preload_act_table(ACT.Exp)
            act.wait_ge(loaded["col"], 16)
            z_scale(0)
            square_norms(0, 0)
            z_scale(1)
            square_norms(0, 1)
            square_norms(1, 0)
            square_norms(1, 1)
            k_first(0, 0)
            k_second(0, 0)
            k_first(0, 1)
            copy_t("x1t", 0, x1_t)
            k_second(0, 1)
            q_first(0)
            q_second(0)
            k_first(1, 0)
            k_second(1, 0)
            copy_t("x1t", 1, x1_t)
            k_first(1, 1)
            k_second(1, 1)
            q_first(1)
            q_second(1)

            act.wait_ge(mask_ready, 1)
            for b in range(B):
                for s in range(STEPS):
                    kt = s % KT
                    e = exp_of(b, s)
                    act.wait_ge(*filled("scores", b, s))
                    if e > NE:
                        act.wait_ge(*used(e - NE - 1))
                    k0 = bank("scores", b, s)
                    nc.scalar.activation(weights[:, (e - 1) % NE], ps[:, k0:k0 + 2, :].rearrange("p a (h s) -> p (a h) s", h=2),
                                         ACT.Exp, scale=SCORE_SCALE,
                                         bias=mask_bias[:, b * KT + kt:b * KT + kt + 1]).then_inc(*take("scores", b, s))
                    if b == 1 and s == STEPS - 1:
                        copy_t("x2t", 0, x2_t)

            nc.scalar.preload_act_table(ACT.Silu)
            act.wait_ge(k3_ready[1], DC)
            pair = [0]

            def silus(b, m):
                act.wait_ge(*filled("gate", b, m))
                pair[0] += 1
                if pair[0] > 2:
                    before = pair[0] - 3
                    act.wait_ge(*taken("up", before // (FC // 2), before % (FC // 2)))
                for i in range(2):
                    last = nc.scalar.activation(silu[:, (pair[0] - 1) % 2, i, :], ps[:, bank("gate", b, m), S * i:S * (i + 1)], ACT.Silu,
                                         scale=col[:, C_GS + 2 * m + i:C_GS + 2 * m + i + 1])
                last.then_inc(*take("gate", b, m))

            for m in range(FC // 2):
                silus(0, m)
            copy_t("x2t", 1, x2_t)
            for m in range(FC // 2):
                silus(1, m)

        @block.vector
        def _(dve):
            steps = [0]

            def link(ins):
                steps[0] += 1
                ins.then_inc(dve_step, 1)
                dve.wait_ge(dve_step, steps[0])

            roots, root_of = [0], [0] * B

            def row_of(start, width=D):
                return row[:, start:start + width].unsqueeze(1).to_broadcast([P, TT, width])

            def moments(b, src, scale=None, eps=EPS, tiles=range(TT)):
                tiles = list(tiles)
                for t in tiles:
                    last = nc.vector.bn_stats(stats[:, b, t, :], src(t))
                link(last)
                for t in tiles:
                    last = nc.vector.bn_aggr(mean_var[:, b, t, :], stats[:, b, t, :])
                link(last)
                a, z_ = tiles[0], tiles[-1] + 1
                nc.vector.tensor_scalar(var_eps[:, b, a:z_], mean_var[:, b, a:z_, 1], 1.0 if scale is None else scale,
                                        eps, ALU.mult, ALU.add).then_inc(var_ready, 1)
                roots[0] += 1
                root_of[b] = roots[0]

            def normalise(b, src, dst, ready, factor=rstd, tiles=range(TT)):
                dve.wait_ge(rstd_ready, root_of[b])
                for t in tiles:
                    nc.vector.tensor_scalar(dst(t), src(t), mean_var[:, b, t, 0:1], factor[:, b, t:t + 1],
                                            ALU.subtract, ALU.mult).then_inc(ready, 1)

            for b in range(B):
                dve.wait_ge(loaded[f"x{b}"], 16)
                moments(b, lambda t: x_sb[:, TT * b + t, :])
                normalise(b, lambda t: x_sb[:, TT * b + t, :], lambda t: z[:, TT * b + t, :], z_ready[b])

            dve.wait_ge(loaded["mask"], 16)
            nc.vector.tensor_scalar(mask_bias[:], mask_sb[:], 0.5, MASKED, ALU.is_le, ALU.mult).then_inc(mask_ready, 1)
            dve.wait_ge(loaded["col"], 16)
            nc.vector.tensor_scalar(res2[:, 0:1], col[:, C_RS:C_RS + 1], 0.0, 0.3, ALU.max, ALU.min).then_inc(res_ready, 1)
            dve.wait_ge(res_ready, 1)
            nc.vector.tensor_tensor(res2[:, 1:2], res2[:, 0:1], res2[:, 0:1], ALU.mult).then_inc(res_ready, 1)

            dve.wait_ge(loaded["row"], 16)
            for t in range(B * TT):
                last = nc.vector.scalar_tensor_tensor(out=x2b[:, t], in0=x_sb[:, t], scalar=2.0,
                                                      in1=row[:, R_BOUT:R_BOUT + D], op0=ALU.mult, op1=ALU.add)
            link(last)

            def kv_bias(b, t):
                dve.wait_ge(*filled("kv", b, t))
                if b > 0 and t == 0:
                    dve.wait_ge(norms_ready[b - 1], 2 * TT)
                nc.vector.tensor_tensor(kv[:, t].rearrange("p a d -> p (a d)"), ps[:, bank("kv", b, t), :],
                                        row[:, R_BKV:R_BKV + 2 * D], ALU.add).then_inc(*take("kv", b, t))

            def cosine_terms(b):
                dve.wait_ge(*taken("kv", b, 0))
                dve.wait_ge(*taken("kv", b, 1))
                for t in range(TT):
                    nc.vector.tensor_tensor(turned[:, t], kv[:, t, :, 0:ROT],
                                            cos[:, t].unsqueeze(1).to_broadcast([P, 2, ROT]), ALU.mult)
                nc.vector.tensor_tensor(kv_prod[:, b, :, ROT:], kv[:, :, 0, ROT:], kv[:, :, 1, ROT:], ALU.mult).then_inc(prod_ready[b], 1)

            def products(b):
                dve.wait_ge(prod_ready[b], 1)
                dve.wait_ge(crossed_ready[b], 1)
                link(nc.vector.tensor_tensor(turned[:], turned[:], crossed[:], ALU.add))
                nc.vector.tensor_tensor(kv_prod[:, b, :, 0:ROT], turned[:, :, 0, :], turned[:, :, 1, :], ALU.mult).then_inc(prod_ready[b], 1)

            def gate_queries(b):
                dve.wait_ge(*filled("a", b))
                nc.vector.tensor_scalar(gate_a[:, b, :], ps[:, bank("a", b), 0:DC], 0.5, 0.5,
                                        ALU.mult, ALU.add).then_inc(*take("a", b))
                dve.wait_ge(*taken("a", b))
                dve.wait_ge(*filled("aq", b))
                for c in range(DC):
                    last = nc.vector.tensor_scalar(aq_t[:, c, S * b:S * (b + 1)], ps[:, bank("aq", b), S * c:S * (c + 1)],
                                            col[:, C_BIN + c:C_BIN + c + 1], gate_a[:, b, c:c + 1],
                                            ALU.add, ALU.mult)
                last.then_inc(*take("aq", b))

            def v_bias(b, n):
                dve.wait_ge(*filled("v", b, n))
                dve.wait_ge(v_ones, b + 1)
                for i in range(2):
                    kt = b * KT + 2 * n + i
                    last = nc.vector.tensor_tensor(v_sb[:, kt, :, 0:HD],
                                            ps[:, bank("v", b, n), D * i:D * (i + 1)].rearrange("p (h d) -> p h d", d=HD),
                                            row[:, R_BV:R_BV + D].rearrange("p (h d) -> p h d", d=HD), ALU.add)
                last.then_inc(*take("v", b, n))

            def stream1_sum(b):
                h1 = x2b[:, TT * b:TT * (b + 1)]
                dve.wait_ge(*filled("y", b))
                nc.vector.tensor_tensor(h1, ps[:, bank("y", b), :].rearrange("p (t d) -> p t d", t=TT), h1,
                                        ALU.add).then_inc(*take("y", b))
                dve.wait_ge(*taken("y", b))
                moments(b, lambda t: x2b[:, TT * b + t, :])

            def stream1_norm(b):
                normalise(b, lambda t: x2b[:, TT * b + t, :], lambda t: x1[:, TT * b + t, :], x1_ready[b])

            def k_remainder(b, c):
                dve.wait_ge(k1_ready[b], c + 1)
                if b > 0:
                    dve.wait_ge(k3_ready[b - 1], c + 1)
                nc.vector.scalar_tensor_tensor(out=k_rest[:, c], in0=ps[:, bank("k", b, c), :],
                                               scalar=col[:, C_BK + c:C_BK + c + 1], in1=k_part[0][:, c],
                                               op0=ALU.add, op1=ALU.subtract).then_inc(*take("k", b, c))

            def k_third(b, c):
                dve.wait_ge(k2_ready[b], c + 1)
                if b > 0:
                    dve.wait_ge(k_stored[b - 1][2], 16)
                nc.vector.tensor_tensor(k_part[2][:, c], k_rest[:, c], k_part[1][:, c], ALU.subtract).then_inc(k3_ready[b], 1)

            def q_remainder(b):
                dve.wait_ge(q1_ready[b], 1)
                if b > 0:
                    dve.wait_ge(q3_ready[b - 1], 1)
                for c in range(DC):
                    last = nc.vector.scalar_tensor_tensor(out=q_rest[:, c], in0=ps[:, bank("q", b), S * c:S * (c + 1)],
                                                          scalar=col[:, C_BQ + c:C_BQ + c + 1], in1=q_part[0][:, c],
                                                          op0=ALU.add, op1=ALU.subtract)
                last.then_inc(*take("q", b))

            def q_third(b):
                dve.wait_ge(q2_ready[b], 1)
                if b > 0:
                    dve.wait_ge(q_stored[b - 1][2], 16)
                nc.vector.tensor_tensor(q_part[2][:], q_rest[:], q_part[1][:], ALU.subtract).then_inc(q3_ready[b], 1)

            dve.wait_ge(loaded["cos"], 16)
            kv_bias(0, 0)
            kv_bias(0, 1)
            cosine_terms(0)
            products(0)
            kv_bias(1, 0)
            kv_bias(1, 1)
            gate_queries(0)
            cosine_terms(1)
            products(1)
            stream1_sum(0)
            k_remainder(0, 0)
            stream1_norm(0)
            gate_queries(1)
            k_remainder(0, 1)
            k_third(0, 0)
            stream1_sum(1)
            k_third(0, 1)
            q_remainder(0)
            stream1_norm(1)
            q_third(0)
            dve.wait_ge(loaded["late_row"], 16)
            v_bias(0, 0)
            v_bias(0, 1)
            k_remainder(1, 0)
            k_third(1, 0)
            k_remainder(1, 1)
            k_third(1, 1)
            q_remainder(1)
            q_third(1)
            v_bias(1, 0)

            def take_pv(b, g):
                n = b * NG + g
                dve.wait_ge(*filled("pv", b, g))
                if n >= 2:
                    dve.wait_ge(*filled("pvt", *divmod(n - 2, NG)))
                nc.vector.tensor_copy(pv_sb[:, n % 2, :], ps[:, bank("pv", b, g), 0:S]).then_inc(*take("pv", b, g))

            def normalise_ctx(b, g):
                dve.wait_ge(*filled("pvt", b, g))
                t_view = ps[:, bank("pvt", b, g), 0:TT * P].rearrange("p (t h r) -> p t h r", t=TT, r=32)
                link(nc.vector.reciprocal(total_inv[:], t_view[:, :, :, HD]))
                for t in range(TT):
                    last = nc.vector.tensor_tensor(
                        ctx_out[:, t, g * HG * HD:(g + 1) * HG * HD].rearrange("p (h d) -> p h d", d=HD),
                        t_view[:, t, :, 0:HD], total_inv[:, t].unsqueeze(2).to_broadcast([P, HG, HD]), ALU.mult)
                last.then_inc(*take("pvt", b, g))

            def take_ctx(b, c):
                dve.wait_ge(*filled("ctxt", b, c))
                if b > 0:
                    dve.wait_ge(*filled("delta", b - 1))
                nc.vector.tensor_copy(ctx_out_t[:, c, :], ps[:, bank("ctxt", b, c), 0:S]).then_inc(*take("ctxt", b, c))

            def stream2_norm(b):
                dve.wait_ge(*filled("delta", b))
                nc.vector.tensor_tensor(delta, ps[:, bank("delta", b), :].rearrange("p (t d) -> p t d", t=TT),
                                        row_of(R_BO), ALU.add).then_inc(*take("delta", b))
                dve.wait_ge(*taken("delta", b))
                moments(b, lambda t: delta[:, t, :], scale=res2[:, 1:2])

            def stream2_scale(b):
                for t in range(TT):
                    last = nc.vector.scalar_tensor_tensor(out=delta[:, t, :], in0=delta[:, t, :], scalar=mean_var[:, b, t, 0:1],
                                                          in1=row[:, R_LG:R_LG + D], op0=ALU.subtract, op1=ALU.mult)
                link(last)

            def stream2_sum(b):
                dve.wait_ge(rstd_ready, root_of[b])
                dve.wait_ge(x1b_ready[b], 1)
                for t in range(TT):
                    last = nc.vector.scalar_tensor_tensor(out=delta[:, t, :], in0=delta[:, t, :], scalar=rstd_rs[:, b, t:t + 1],
                                                          in1=x1b[:, TT * b + t], op0=ALU.mult, op1=ALU.add)
                link(last)

            def stream2_moments(b):
                moments(b, lambda t: delta[:, t, :])

            def stream2(b):
                normalise(b, lambda t: delta[:, t, :], lambda t: x2[:, TT * b + t, :], x2_ready[b])

            dve.wait_ge(res_ready, 2)
            for b in range(B):
                for s in range(STEPS):
                    e = exp_of(b, s)
                    dve.wait_ge(*taken("scores", b, s))
                    w = weights[:, (e - 1) % NE].rearrange("p h s -> p (h s)")
                    nc.vector.tensor_scalar(w, w, E_HIGH, E_LOW, ALU.min, ALU.max).then_inc(clipped, 1)
                    if b == 0 and s == 1:
                        v_bias(1, 1)
                    g = s // KT - 1
                    if s % KT == 0:
                        if g >= 0:
                            take_pv(b, g)
                        elif b > 0:
                            take_pv(b - 1, NG - 1)
                    if g >= 0 and s % KT == 2:
                        normalise_ctx(b, g)
                    if s % KT == 0 and g == 2:
                        take_ctx(b, 0)
                    if b > 0 and s == 2:
                        normalise_ctx(b - 1, NG - 1)
                    if b > 0 and s == 4:
                        take_ctx(b - 1, 1)
                    if b > 0 and s == 7:
                        stream2_norm(b - 1)
                    if b > 0 and s == 9:
                        stream2_scale(b - 1)
                    if b > 0 and s == 10:
                        stream2_sum(b - 1)
                    if b > 0 and s == 11:
                        stream2_moments(b - 1)
                    if b > 0 and s == 13:
                        stream2(b - 1)
            take_pv(1, NG - 1)
            normalise_ctx(1, NG - 1)

            pair = [0]

            def gated(b, m):
                dve.wait_ge(*filled("up", b, m))
                pair[0] += 1
                dve.wait_ge(*taken("gate", b, m))
                if b > 0:
                    dve.wait_ge(*filled("down", b - 1, TT - 1))
                for i in range(2):
                    last = nc.vector.scalar_tensor_tensor(out=hidden[:, 2 * m + i, :], in0=ps[:, bank("up", b, m), S * i:S * (i + 1)],
                                                   scalar=col[:, C_US + 2 * m + i:C_US + 2 * m + i + 1],
                                                   in1=silu[:, (pair[0] - 1) % 2, i, :], op0=ALU.mult,
                                                   op1=ALU.mult)
                last.then_inc(*take("up", b, m))

            def output(b, tiles):
                tiles = list(tiles)
                dve.wait_ge(*((x2_ready[B - 1], TT) if b == 0 else (final_ready, TT * b)))
                for t in tiles:
                    dve.wait_ge(*filled("down", b, t))
                    nc.vector.tensor_tensor(delta[:, t, :], ps[:, bank("down", b, t), 0:D], x2[:, TT * b + t, :],
                                            ALU.add).then_inc(*take("down", b, t))
                for t in tiles:
                    dve.wait_ge(*taken("down", b, t))
                moments(b, lambda t: delta[:, t, :], tiles=tiles)
                normalise(b, lambda t: delta[:, t, :], lambda t: final[:, TT * b + t, :], final_ready, tiles=tiles)

            take_ctx(1, 1)
            gated(0, 0)
            stream2_norm(1)
            stream2_scale(1)
            stream2_sum(1)
            stream2_moments(1)
            gated(0, 1)
            stream2(1)
            gated(0, 2)
            output(0, range(TT))
            for m in range(FC // 2):
                gated(1, m)
            for t in range(TT):
                output(1, [t])

        @block.tensor
        def _(pe):
            done = []

            def begin(*job):
                assert ORDER[len(done)] == job, (ORDER[len(done)], job)
                done.append(job)
                for earlier in PLAN.before[job]:
                    pe.wait_ge(*taken(*earlier))

            def transposes(job, src, ready, need):
                begin(*job)
                pe.wait_ge(ready, need)
                for c in range(DC):
                    for t in range(TT):
                        last = nc.tensor.transpose(ps[:, bank(*job), S * c + P * t:S * c + P * (t + 1)],
                                                   src[:, TT * job[1] + t, P * c:P * (c + 1)], ident[:])
                last.then_inc(*full(*job))

            def k_proj(b, c):
                begin("k", b, c)
                for i in range(DC):
                    last = nc.tensor.matmul(ps[:, bank("k", b, c), :], wk_sb[:, i, P * c:P * (c + 1)],
                                            ctx_sb[:, i, T * b:T * (b + 1)], start=(i == 0), stop=(i == DC - 1))
                last.then_inc(*full("k", b, c))

            def kv_proj(b, t):
                begin("kv", b, t)
                n = TT * b + t
                for i in range(DC):
                    last = nc.tensor.matmul(ps[:, bank("kv", b, t), :], z_t[:, i, P * n:P * (n + 1)],
                                            w_in_sb[:, i, D:3 * D], start=(i == 0), stop=(i == DC - 1))
                last.then_inc(*full("kv", b, t))

            def feature_proj(job, w, src):
                b = job[1]
                begin(*job)
                for c in range(DC):
                    for i in range(DC):
                        last = nc.tensor.matmul(ps[:, bank(*job), S * c:S * (c + 1)], w[:, i, P * c:P * (c + 1)],
                                                src[:, i, S * b:S * (b + 1)], start=(i == 0), stop=(i == DC - 1))
                last.then_inc(*full(*job))

            def token_proj(job, w, src, offset):
                begin(*job)
                for t in range(TT):
                    for i in range(DC):
                        last = nc.tensor.matmul(ps[:, bank(*job), D * t:D * (t + 1)],
                                                src[:, i, offset + P * t:offset + P * (t + 1)], w[:, i, :],
                                                start=(i == 0), stop=(i == DC - 1))
                last.then_inc(*full(*job))

            def similarity(b):
                begin("a", b)
                pe.wait_ge(prod_ready[b], 2)
                pe.wait_ge(pair_ready[b], 1)
                for c in range(DC):
                    for t in range(TT):
                        last = nc.tensor.matmul(ps[:, bank("a", b), c:c + 1], kv_prod[:, b, t, P * c:P * (c + 1)],
                                                pair_inv[:, b, t:t + 1], start=(t == 0), stop=(t == TT - 1))
                last.then_inc(*full("a", b))

            def y_proj(b):
                pe.wait_ge(*taken("aq", b))
                token_proj(("y", b), w_out_sb, aq_t, S * b)

            def q_proj(b):
                pe.wait_ge(*taken("x1t", b))
                feature_proj(("q", b), wq_sb, x1_t)

            pe.wait_ge(ident_ready, 1)
            for _ in range(WARM_UP):
                nc.tensor.transpose(ps[:, 7, 0:P], ident[:], ident[:])
            transposes(("zt", 0), z, z_ready[0], 2)
            pe.wait_ge(loaded["w_kv"], 16)
            pe.wait_ge(*taken("zt", 0))
            kv_proj(0, 0)
            kv_proj(0, 1)
            transposes(("zt", 1), z, z_ready[1], 2)
            pe.wait_ge(loaded["w_q"], 16)
            feature_proj(("aq", 0), w_in_sb, z_t)
            pe.wait_ge(*taken("zt", 1))
            kv_proj(1, 0)
            kv_proj(1, 1)
            similarity(0)
            feature_proj(("aq", 1), w_in_sb, z_t)
            pe.wait_ge(loaded["w_out"], 16)
            y_proj(0)
            pe.wait_ge(loaded["wk"], 16)
            pe.wait_ge(loaded["ctx0"], 16)
            k_proj(0, 0)
            similarity(1)
            k_proj(0, 1)
            transposes(("x1t", 0), x1, x1_ready[0], 2)
            y_proj(1)
            pe.wait_ge(loaded["wq"], 16)
            q_proj(0)
            pe.wait_ge(loaded["wv"], 16)
            token_proj(("v", 0, 0), wv_sb, ctx_sb, 0)
            token_proj(("v", 0, 1), wv_sb, ctx_sb, S)
            pe.wait_ge(loaded["ctx1"], 16)
            k_proj(1, 0)
            transposes(("x1t", 1), x1, x1_ready[1], 2)
            k_proj(1, 1)
            q_proj(1)
            token_proj(("v", 1, 0), wv_sb, ctx_sb, T)

            def scores(b, s):
                g, kt = divmod(s, KT)
                begin("scores", b, s)
                if s == 0:
                    pe.wait_ge(k_stacked[b], 16 * 3)
                    pe.wait_ge(q_stacked_first[b], 16 * 2)
                if s == KT:
                    pe.wait_ge(q_stacked_rest[b], 16 * 2)
                k0 = bank("scores", b, s)
                for j in range(HG):
                    h = g * HG + j
                    last = nc.tensor.matmul(ps[:, k0 + j // 2, S * (j % 2):S * (j % 2 + 1)],
                                            k_stack[:, b, h, P * kt:P * (kt + 1)],
                                            q_stack[:, b, h, :], start=True, stop=True)
                last.then_inc(*full("scores", b, s))

            def weigh(b, s):
                g, kt = divmod(s, KT)
                e = exp_of(b, s)
                if kt == 0:
                    begin("pv", b, g)
                pe.wait_ge(clipped, e)
                for j in range(HG):
                    last = nc.tensor.matmul(ps[32 * j:32 * (j + 1), bank("pv", b, g), 0:S],
                                            v_sb[:, b * KT + kt, g * HG + j, :], weights[:, (e - 1) % NE, j, :],
                                            start=(kt == 0), stop=(kt == KT - 1))
                last.then_inc(*(full("pv", b, g) if kt == KT - 1 else (weights_used, 1)))

            def transpose_pv(b, g):
                n = b * NG + g
                begin("pvt", b, g)
                pe.wait_ge(*taken("pv", b, g))
                for t in range(TT):
                    last = nc.tensor.transpose(ps[:, bank("pvt", b, g), P * t:P * (t + 1)],
                                               pv_sb[:, n % 2, P * t:P * (t + 1)], ident[:])
                last.then_inc(*full("pvt", b, g))

            def transpose_ctx(b, c):
                begin("ctxt", b, c)
                pe.wait_ge(*taken("pvt", b, 2 * c))
                pe.wait_ge(*taken("pvt", b, 2 * c + 1))
                for t in range(TT):
                    last = nc.tensor.transpose(ps[:, bank("ctxt", b, c), P * t:P * (t + 1)],
                                               ctx_out[:, t, P * c:P * (c + 1)], ident[:])
                last.then_inc(*full("ctxt", b, c))

            def out_proj(b):
                pe.wait_ge(*taken("ctxt", b, 0))
                pe.wait_ge(*taken("ctxt", b, 1))
                token_proj(("delta", b), wo_sb, ctx_out_t, 0)

            follow = {"pvt": transpose_pv, "ctxt": transpose_ctx, "delta": out_proj,
                      "x2t": lambda b: transposes(("x2t", b), x2, x2_ready[b], 2)}
            pe.wait_ge(loaded["wo"], 16)
            scores(0, 0)
            scores(0, 1)
            token_proj(("v", 1, 1), wv_sb, ctx_sb, T + S)
            for b in range(B):
                pe.wait_ge(*taken("v", b, 0))
                pe.wait_ge(*taken("v", b, 1))
                for s in range(STEPS):
                    if s + 2 < STEPS:
                        scores(b, s + 2)
                    elif b + 1 < B:
                        scores(b + 1, s + 2 - STEPS)
                    weigh(b, s)
                    for job in after_weigh(b, s):
                        follow[job[0]](*job[1:])
            transpose_pv(1, NG - 1)

            def inner(kind, w, b, m):
                begin(kind, b, m)
                for i in range(2):
                    f = 2 * m + i
                    for c in range(DC):
                        last = nc.tensor.matmul(ps[:, bank(kind, b, m), S * i:S * (i + 1)], w[:, c, P * f:P * (f + 1)],
                                                x2_t[:, c, S * b:S * (b + 1)], start=(c == 0), stop=(c == DC - 1))
                last.then_inc(*full(kind, b, m))

            def down(b, t):
                begin("down", b, t)
                for f in range(FC):
                    pe.wait_ge(*taken("up", b, f // 2))
                    last = nc.tensor.matmul(ps[:, bank("down", b, t), 0:D], hidden[:, f, P * t:P * (t + 1)],
                                            down_sb[:, f, :], start=(f == 0), stop=(f == FC - 1))
                last.then_inc(*full("down", b, t))

            pe.wait_ge(loaded["gate"], 16)
            pe.wait_ge(loaded["up"], 16)
            pe.wait_ge(*taken("x2t", 0))
            inner("gate", gate_sb, 0, 0)
            transpose_ctx(1, 1)
            inner("up", up_sb, 0, 0)
            out_proj(1)
            inner("gate", gate_sb, 0, 1)
            inner("up", up_sb, 0, 1)
            inner("gate", gate_sb, 0, 2)
            inner("up", up_sb, 0, 2)
            pe.wait_ge(down_scaled, 1)
            down(0, 0)
            transposes(("x2t", 1), x2, x2_ready[1], 2)
            down(0, 1)
            pe.wait_ge(*taken("x2t", 1))
            for m in range(FC // 2):
                inner("gate", gate_sb, 1, m)
                inner("up", up_sb, 1, m)
            down(1, 0)
            down(1, 1)


def kernel(x, ctx_2048, mask_BxS2_ik0, L0_attn_W_in, L0_attn_b_in, L0_attn_W_out, L0_attn_b_out,
           L0_attn_gamma, L0_attn_beta, L0_xattn_Wq, L0_xattn_bq, L0_xattn_Wk, L0_xattn_bk, L0_xattn_Wv,
           L0_xattn_bv, L0_xattn_Wo, L0_xattn_bo, L0_xattn_ln_gamma, L0_xattn_ln_beta,
           L0_xattn_residual_scale, L0_ffn_gate_w, L0_ffn_up_w, L0_ffn_down_w, L0_ffn_gate_s,
           L0_ffn_up_s, L0_ffn_down_s):
    import concourse.bacc as bacc
    from concourse.bass_utils import run_bass_kernel_spmd

    f32 = np.float32

    def chunked(a):
        return np.asarray(a).reshape(-1, P).T

    def padded(a):
        a = np.asarray(a)
        return np.concatenate([a, np.zeros((FC * P - a.shape[0],) + a.shape[1:], a.dtype)])

    def heads_paired(a):
        a = np.asarray(a)
        return a.reshape(NH // DC, DC, HD, -1).transpose(1, 0, 2, 3).reshape(a.shape)

    cols = np.concatenate([chunked(L0_attn_gamma), chunked(L0_attn_beta), chunked(np.asarray(L0_attn_b_in)[:D]),
                           chunked(heads_paired(L0_xattn_bq)), chunked(heads_paired(L0_xattn_bk)), chunked(padded(L0_ffn_gate_s)),
                           chunked(padded(L0_ffn_up_s)),
                           np.broadcast_to(np.asarray(L0_xattn_residual_scale), (P, 1))], axis=1)
    rows = np.concatenate([np.asarray(a) for a in (
        np.asarray(L0_attn_b_in)[D:], L0_attn_b_out, L0_xattn_bv, L0_xattn_bo, L0_xattn_ln_gamma,
        L0_xattn_ln_beta, L0_ffn_down_s)])[None]
    inv_freq = f32(1.0) / f32(10000.0) ** (np.arange(0, ROT, 2, dtype=f32) / f32(ROT))
    angle = np.repeat(np.arange(S, dtype=f32)[:, None] * inv_freq[None, :], 2, axis=1)
    sign = np.tile(np.array([-1.0, 1.0], f32), ROT // 2)
    arrays = {
        "x": np.asarray(x).reshape(B * S, D),
        "ctx_t": np.asarray(ctx_2048).reshape(B * T, D).T,
        "mask_cols": np.asarray(mask_BxS2_ik0).reshape(B * KT, P).T,
        "cols": cols,
        "rows": rows,
        "rope_cos": np.cos(angle).astype(f32),
        "rope_sin": (np.sin(angle) * sign).astype(f32),
        "w_in": np.asarray(L0_attn_W_in),
        "w_out": np.asarray(L0_attn_W_out),
        "wq_t": heads_paired(L0_xattn_Wq).T,
        "wk_t": heads_paired(L0_xattn_Wk).T,
        "wv_t": np.asarray(L0_xattn_Wv).T,
        "wo_t": np.asarray(L0_xattn_Wo).T,
        "gate_t": padded(L0_ffn_gate_w).T,
        "up_t": padded(L0_ffn_up_w).T,
        "down_t": padded(np.asarray(L0_ffn_down_w).T),
    }
    arrays = {name: np.ascontiguousarray(a) for name, a in arrays.items()}

    nc = bacc.Bacc("TRN2", target_bir_lowering=False, num_devices=1)
    args = [nc.dram_tensor(name, a.shape, mybir.dt.from_np(a.dtype), kind="ExternalInput").ap()
            for name, a in arrays.items()]
    out = nc.dram_tensor("out", (B * S, D), F32, kind="ExternalOutput").ap()
    decoder_layer(nc, *args, out)
    result = run_bass_kernel_spmd(nc, [arrays], core_ids=[0])
    return result.results[0]["out"].reshape(B, S, D)
```

```python
from contextlib import ExitStack

import numpy as np

import concourse.bass as bass
from concourse import mybir

ALU = mybir.AluOpType
ACT = mybir.ActivationFunctionType
F32 = mybir.dt.float32
BF16 = mybir.dt.bfloat16
F32R = mybir.dt.float32r
I32 = mybir.dt.int32

P = 128
B = 2
S = 256
T = 512
D = 256
ROT = D // 2
DC = D // P
TT = S // P
KT = T // P
NH = 16
HD = D // NH
HG = 4
NG = NH // HG
FC = 6
EPS = 1e-5
SCORE_SCALE = 1.0 / np.sqrt(HD)
E_LOW = float(np.exp(np.float32(-50.0)))
E_HIGH = float(np.exp(np.float32(50.0)))
MASKED = -3.0e38
STEPS = NG * KT
NE = 4
PROB_EPS = 1e-8
DOWN_RUN = FC // 2
WARM_UP = 20
HIGH_LOW = ("high", "low")
HL_PAIRS = ((0, 0), (0, 1), (1, 0))
Q_PARTS = (0, 1, 2, 0, 1, 2, 0, 1)
K_PARTS = (0, 0, 0, 1, 1, 1, 2, 2)

C_GAMMA, C_BETA, C_BIN, C_BQ, C_BK, C_GS, C_US, C_RS = 0, 2, 4, 6, 8, 10, 16, 22
NCOL = 23
R_BKV, R_BOUT, R_BV, R_BO, R_LG, R_LB, R_DS = 0, 512, 768, 1024, 1280, 1536, 1792
NROW = 2048


class Plan:

    def __init__(self, jobs):
        self.at = {}
        self.before = {}
        count = [0] * 8
        last = {}
        for name, banks in jobs:
            count[banks[0]] += 1
            self.at[name] = (banks, count[banks[0]])
            self.before[name] = []
            for k in banks:
                if k in last and last[k] not in self.before[name]:
                    self.before[name].append(last[k])
                last[k] = name


def after_weigh(b, s):
    jobs = []
    g = s // KT - 1
    if s % KT == 1 and g >= 0:
        jobs.append(("pvt", b, g))
    if s % KT == 3 and g == 1:
        jobs.append(("ctxt", b, 0))
    if b > 0:
        jobs += {1: [("pvt", b - 1, NG - 1)], 3: [("ctxt", b - 1, 1)], 5: [("delta", b - 1)],
                 13: [("x2t", b - 1)]}.get(s, [])
    return jobs


def after_weigh_bank(job):
    return 6 + job[-1] % 2 if job[0] == "pvt" else 7


def plan():
    jobs = [
        (("zt", 0, 0), [0]), (("zt", 0, 1), [7]), (("kv", 0, 0), [1]), (("kv", 0, 1), [2]),
        (("zt", 1, 0), [3]), (("zt", 1, 1), [0]), (("aq", 0), [4]),
        (("kv", 1, 0), [5]), (("a", 0), [0]), (("kv", 1, 1), [6]), (("y", 0), [1]), (("aq", 1), [7]),
        (("k", 0, 0), [2]), (("a", 1), [3]), (("x1t", 0), [5]), (("k", 0, 1), [0]),
        (("q", 0), [4]), (("y", 1), [6]), (("v", 0, 0), [1]), (("v", 0, 1), [7]), (("k", 1, 0), [2]),
        (("k", 1, 1), [0]), (("v", 1, 0), [6]), (("v", 1, 1), [4]), (("x1t", 1), [3]),
    ]
    steps = [(b, s) for b in range(B) for s in range(STEPS)]
    jobs += [(("scores",) + steps[n], [2 * (n % 2), 2 * (n % 2) + 1]) for n in range(2)]
    jobs += [(("q", 1), [7])]
    for n, (b, s) in enumerate(steps):
        if n + 2 < len(steps):
            jobs.append((("scores",) + steps[n + 2], [2 * (n % 2), 2 * (n % 2) + 1]))
        g = s // KT
        if s % KT == 0:
            jobs.append((("pv", b, g), [4 + g % 2]))
        for job in after_weigh(b, s):
            jobs.append((job, [after_weigh_bank(job)]))
    jobs += [(("gate", 0, 0), [0]), (("pvt", 1, NG - 1), [6]), (("gate", 0, 1), [1]), (("ctxt", 1, 1), [7]),
             (("up", 0, 0), [2]), (("delta", 1), [6]), (("up", 0, 1), [3]), (("gate", 0, 2), [0]), (("up", 0, 2), [2]),
             (("down", 0, 0), [4]), (("down", 0, 1), [5]), (("x2t", 1), [7]),
             (("gate", 1, 0), [1]), (("gate", 1, 1), [0]), (("up", 1, 0), [3]), (("up", 1, 1), [2]),
             (("gate", 1, 2), [1]), (("up", 1, 2), [3]), (("down", 1, 0), [6]), (("down", 1, 1), [7])]
    return Plan(jobs), [name for name, _ in jobs]


PLAN, ORDER = plan()


def decoder_layer(nc, x, ctx_t, mask_cols, cols, rows, rope_cos, rope_sin, w_in, w_out,
                  wq_t, wk_t, wv_t, wo_t, gate_t, up_t, down_t, out):
    with ExitStack() as stack:
        def sb(name, shape, dt=F32):
            return stack.enter_context(nc.sbuf_tensor(name, shape, dt))

        def sem(name):
            return stack.enter_context(nc.semaphore(name))

        def per_batch(name):
            return [sem(f"{name}{b}") for b in range(B)]

        wo_sb = sb("wo_sb", [P, DC, D])
        gate_hl = [sb(f"gate_{n}", [P, DC, FC * P], F32R) for n in HIGH_LOW]
        up_hl = [sb(f"up_{n}", [P, DC, FC * P], F32R) for n in HIGH_LOW]
        down_hl = [sb(f"down_{n}", [P, FC, D], F32R) for n in HIGH_LOW]
        col = sb("col", [P, NCOL])
        row = sb("row", [P, NROW])
        mask_sb = sb("mask_sb", [P, B * KT], I32)
        mask_bias = sb("mask_bias", [P, B * KT])
        ident = sb("ident", [P, P])
        power = sb("power", [P, 4])
        res2 = sb("res2", [P, 2])
        x_sb = sb("x_sb", [P, B * TT, D])
        x2b = sb("x2b", [P, B * TT, D])
        stats = sb("stats", [P, B, TT, 6])
        mean_var = sb("mean_var", [P, B, TT, 2])
        var_eps = sb("var_eps", [P, B, TT])
        rstd = sb("rstd", [P, B, TT])
        rstd_rs = sb("rstd_rs", [P, B, TT])
        z = sb("z", [P, B * TT, D])
        turned = sb("turned", [P, TT, 2, ROT])
        crossed = sb("crossed", [P, TT, 2, ROT])
        norm_sq = sb("norm_sq", [P, B, TT, 2])
        norm_inv = sb("norm_inv", [P, B, TT, 2])
        pair_inv = sb("pair_inv", [P, B, TT])
        gate_a = sb("gate_a", [P, B, DC])
        x1 = sb("x1", [P, B * TT, D])
        k_rest = sb("k_rest", [P, DC, T])
        k_part = [sb(f"k_part{i}", [P, DC, T], BF16) for i in range(3)]
        q_rest = sb("q_rest", [P, DC, S])
        q_part = [sb(f"q_part{i}", [P, DC, S], BF16) for i in range(3)]
        q_stack = [sb("q_stack0", [P, NH, S], BF16)]
        v_sb = sb("v_sb", [P, B * KT, NH, 32])
        total_inv = sb("total_inv", [P, TT, HG])
        with ExitStack() as early:
            def early_sb(name, shape, dt=F32):
                return early.enter_context(nc.sbuf_tensor(name, shape, dt))

            z_t, w_in_sb = early_sb("z_t", [P, DC, B * S]), early_sb("w_in_sb", [P, DC, 3 * D])
            kv, kv_prod = early_sb("kv", [P, TT, 2, D]), early_sb("kv_prod", [P, B, TT, D])
            aq_t = early_sb("aq_t", [P, DC, B * S])
            ctx_sb = early_sb("ctx_sb", [P, DC, B * T])
            wk_sb = early_sb("wk_sb", [P, DC, D])
            squares = early_sb("squares", [P, TT, 2, D], BF16)
            x1_t = early_sb("x1_t", [P, DC, B * S])
            ctx_hl = [early_sb(f"ctx_{n}", [P, DC, B * T], F32R) for n in HIGH_LOW]
            wk_hl = [early_sb(f"wk_{n}", [P, DC, D], F32R) for n in HIGH_LOW]
            wv_hl = [early_sb(f"wv_{n}", [P, DC, D], F32R) for n in HIGH_LOW]
            w_out_sb, wq_sb = early_sb("w_out_sb", [P, DC, D]), early_sb("wq_sb", [P, DC, D])
            wv_sb = early_sb("wv_sb", [P, DC, D])
            cos, sin = early_sb("cos", [P, TT, ROT]), early_sb("sin", [P, TT, ROT])
            down_sb = early_sb("down_sb", [P, FC, D])
            gate_sb, up_sb = early_sb("gate_sb", [P, DC, FC * P]), early_sb("up_sb", [P, DC, FC * P])
        k_stack = [sb("k_stack0", [P, NH, T], BF16)]
        pv_sb = sb("pv_sb", [P, 2, S])
        weights = sb("weights", [P, NE, HG, S])
        x2_hl = [sb(f"x2_{n}", [P, DC, S], F32R) for n in HIGH_LOW]
        hidden_hl = [sb(f"hidden_{n}", [P, FC, S], F32R) for n in HIGH_LOW]
        ctx_out_t = sb("ctx_out_t", [P, DC, S])
        k_stack.append(sb("k_stack1", [P, NH, T], BF16))
        q_stack.append(sb("q_stack1", [P, NH, S], BF16))
        ctx_out = crossed[:].rearrange("p t a r -> p t (a r)")
        delta = turned[:].rearrange("p t a r -> p t (a r)")
        x2 = x2b[:]
        x1b = x_sb[:]
        silu = k_rest[:].rearrange("p c (a s) -> p c a s", a=2)
        final = z[:]

        ps = stack.enter_context(nc.psum_tensor("ps", [P, 8, 512], F32))
        q_scratch = nc.dram_tensor("q_scratch", (B, 3, HD, NH, S), BF16, kind="Internal").ap()
        k_scratch = nc.dram_tensor("k_scratch", (B, 3, HD, NH, T), BF16, kind="Internal").ap()

        loaded = {n: sem(f"loaded_{n}") for n in
                  ("x0", "x1", "col", "row", "late_row", "cos", "sin", "mask", "ctx0", "ctx1", "wk", "wv",
                   "w_kv", "w_q", "w_out", "wq", "wo", "gate", "up", "down")}
        bank_filled = [sem(f"bank_filled{k}") for k in range(8)]
        bank_taken = [sem(f"bank_taken{k}") for k in range(8)]
        const_ready = sem("const_ready")
        ident_ready = sem("ident_ready")
        mask_ready = sem("mask_ready")
        res_ready = sem("res_ready")
        v_ones = sem("v_ones")
        var_ready = sem("var_ready")
        rstd_ready = sem("rstd_ready")
        dve_step = sem("dve_step")
        pool_step = sem("pool_step")
        z_ready = per_batch("z_ready")
        crossed_ready = per_batch("crossed_ready")
        prod_ready = per_batch("prod_ready")
        norms_ready, pair_ready = per_batch("norms_ready"), per_batch("pair_ready")
        x1_ready, x1b_ready, x2_ready = per_batch("x1_ready"), per_batch("x1b_ready"), per_batch("x2_ready")
        k1_ready, k2_ready, k3_ready = per_batch("k1_ready"), per_batch("k2_ready"), per_batch("k3_ready")
        q1_ready, q2_ready, q3_ready = per_batch("q1_ready"), per_batch("q2_ready"), per_batch("q3_ready")
        k_stored = [[sem(f"k_stored{b}{i}") for i in range(3)] for b in range(B)]
        q_stored = [[sem(f"q_stored{b}{i}") for i in range(3)] for b in range(B)]
        stacked_first, stacked_rest = per_batch("stacked_first"), per_batch("stacked_rest")
        clipped = sem("clipped")
        weights_used = sem("weights_used")
        down_rows_scaled, down_scaled = sem("down_rows_scaled"), sem("down_scaled")
        gate_high_ready, gate_low_ready = sem("gate_high_ready"), sem("gate_low_ready")
        up_high_ready, up_low_ready = sem("up_high_ready"), sem("up_low_ready")
        down_high_ready, down_low_ready = sem("down_high_ready"), sem("down_low_ready")
        ctx_high_ready, ctx_low_ready = per_batch("ctx_high_ready"), per_batch("ctx_low_ready")
        wk_high_ready, wk_low_ready = sem("wk_high_ready"), sem("wk_low_ready")
        wv_high_ready, wv_low_ready = sem("wv_high_ready"), sem("wv_low_ready")
        x2_high_ready = sem("x2_high_ready")
        hidden_high_ready, hidden_low_ready = sem("hidden_high_ready"), sem("hidden_low_ready")
        delta_centred, delta_summed = sem("delta_centred"), sem("delta_summed")
        last_stats, last_mean = sem("last_stats"), sem("last_mean")
        final_ready = sem("final_ready")
        stored = sem("stored")

        def filled(*job):
            banks, n = PLAN.at[job]
            return bank_filled[banks[0]], n

        def taken(*job):
            banks, n = PLAN.at[job]
            return bank_taken[banks[0]], n

        def bank(*job):
            return PLAN.at[job][0][0]

        def full(*job):
            return bank_filled[bank(*job)], 1

        def take(*job):
            return bank_taken[bank(*job)], 1

        def used(n):
            if n % KT == KT - 1:
                return filled("pv", *divmod(n // KT, NG))
            return weights_used, n - n // KT + 1

        def exp_of(b, s):
            return b * STEPS + s + 1

        block = stack.enter_context(nc.Block())

        @block.sync
        def _(sp):
            def by_chunk(a):
                return a.rearrange("(c p) n -> p c n", p=P)

            def batch(b, n):
                return slice(n * b, n * (b + 1))

            x_v = x.rearrange("(t p) d -> p t d", p=P)
            sp.dma_start(x_sb[:, batch(0, TT)], x_v[:, batch(0, TT)]).then_inc(loaded["x0"], 16)
            sp.dma_start(w_in_sb[:, :, D:], by_chunk(w_in)[:, :, D:]).then_inc(loaded["w_kv"], 16)
            sp.dma_start(x_sb[:, batch(1, TT)], x_v[:, batch(1, TT)]).then_inc(loaded["x1"], 16)
            sp.dma_start(row[:, 0:R_BV], rows[:, 0:R_BV].to_broadcast([P, R_BV])).then_inc(loaded["row"], 16)
            sp.dma_start(cos[:], rope_cos.rearrange("(t p) d -> p t d", p=P)).then_inc(loaded["cos"], 16)
            sp.dma_start(sin[:], rope_sin.rearrange("(t p) d -> p t d", p=P)).then_inc(loaded["sin"], 16)
            sp.dma_start(w_in_sb[:, :, 0:D], by_chunk(w_in)[:, :, 0:D]).then_inc(loaded["w_q"], 16)
            sp.dma_start(w_out_sb[:], by_chunk(w_out)).then_inc(loaded["w_out"], 16)
            sp.dma_start(wk_sb[:], by_chunk(wk_t)).then_inc(loaded["wk"], 16)
            sp.dma_start(ctx_sb[:, :, batch(0, T)], by_chunk(ctx_t)[:, :, batch(0, T)]).then_inc(loaded["ctx0"], 16)
            sp.dma_start(wq_sb[:], by_chunk(wq_t)).then_inc(loaded["wq"], 16)
            sp.dma_start(wv_sb[:], by_chunk(wv_t)).then_inc(loaded["wv"], 16)
            sp.dma_start(row[:, R_BV:], rows[:, R_BV:].to_broadcast([P, NROW - R_BV])).then_inc(loaded["late_row"], 16)
            sp.dma_start(ctx_sb[:, :, batch(1, T)], by_chunk(ctx_t)[:, :, batch(1, T)]).then_inc(loaded["ctx1"], 16)
            sp.dma_start(wo_sb[:], by_chunk(wo_t)).then_inc(loaded["wo"], 16)
            sp.dma_start(gate_sb[:], by_chunk(gate_t)).then_inc(loaded["gate"], 16)
            sp.dma_start(up_sb[:], by_chunk(up_t)).then_inc(loaded["up"], 16)
            sp.dma_start(down_sb[:], by_chunk(down_t)).then_inc(loaded["down"], 16)

            def store_part(scratch, part, i, b, stored_):
                sp.dma_start(scratch[b, i].rearrange("d (h c) t -> h d (c t)", c=DC),
                             part[i][:].rearrange("p c t -> p (c t)")).then_inc(stored_[b][i], 16)

            def store_k(b, i):
                sp.wait_ge([k1_ready, k2_ready, k3_ready][i][b], DC)
                store_part(k_scratch, k_part, i, b, k_stored)

            def store_q(b, i):
                sp.wait_ge([q1_ready, q2_ready, q3_ready][i][b], 1)
                store_part(q_scratch, q_part, i, b, q_stored)

            def stack_k(b, i, h, done):
                n, blocks = K_PARTS.index(i), K_PARTS.count(i)
                sp.wait_ge(k_stored[b][i], 16)
                sp.dma_start(k_stack[b][HD * n:HD * (n + blocks), h].rearrange("p h t -> p (h t)"),
                             k_scratch[b, i, :, h].rearrange("d h t -> d (h t)").unsqueeze(0).to_broadcast(
                                 [blocks, HD, (h.stop - h.start) * T])).then_inc(done, 16)

            def stack_q(b, h, done):
                for i in range(3):
                    sp.wait_ge(q_stored[b][i], 16)
                for rows, times, parts in ((slice(0, 6 * HD), 2, 3), (slice(6 * HD, P), 1, 2)):
                    src = q_scratch[b, 0:parts, :, h].rearrange("i d h t -> (i d) (h t)")
                    if times > 1:
                        src = src.unsqueeze(0).to_broadcast([times, parts * HD, (h.stop - h.start) * S])
                    sp.dma_start(q_stack[b][rows, h].rearrange("p h t -> p (h t)"), src).then_inc(done, 16)

            first, rest = slice(0, HG), slice(HG, NH)
            store_k(0, 0)
            store_k(0, 1)
            store_q(0, 0)
            store_k(0, 2)
            sp.wait_ge(*filled("a", 1))
            stack_k(0, 0, first, stacked_first[0])
            store_q(0, 1)
            store_q(0, 2)
            stack_k(0, 1, first, stacked_first[0])
            stack_k(0, 2, first, stacked_first[0])
            stack_k(0, 0, rest, stacked_rest[0])
            stack_q(0, first, stacked_first[0])
            stack_k(0, 1, rest, stacked_rest[0])
            stack_k(0, 2, rest, stacked_rest[0])
            stack_q(0, rest, stacked_rest[0])
            for i in range(3):
                store_k(1, i)
            sp.wait_ge(down_low_ready, FC // DOWN_RUN)
            sp.wait_ge(gate_low_ready, DC)
            sp.wait_ge(*filled("q", 1))
            for h, done in ((first, stacked_first[1]), (rest, stacked_rest[1])):
                for i in range(3):
                    stack_k(1, i, h, done)
            for i in range(3):
                store_q(1, i)
            stack_q(1, first, stacked_first[1])
            stack_q(1, rest, stacked_rest[1])
            for n in range(B * TT):
                sp.wait_ge(final_ready, n + 1)
                sp.dma_start(out[n * P:(n + 1) * P, :], final[:, n, :]).then_inc(stored, 16)
            sp.wait_ge(stored, 16 * B * TT)

        @block.gpsimd
        def _(pool):
            steps = [0]

            def link(ins):
                steps[0] += 1
                ins.then_inc(pool_step, 1)
                pool.wait_ge(pool_step, steps[0])

            nc.gpsimd.memset(power[:], -0.5).then_inc(const_ready, 1)
            link(nc.gpsimd.memset(ident[:], 0.0))
            nc.gpsimd.affine_select(out=ident[:], in_=ident[:], compare_op=ALU.not_equal, fill=1.0, base=0,
                                    pattern=[[-1, P]], channel_multiplier=1).then_inc(ident_ready, 1)
            pool.wait_ge(const_ready, 1)

            uses = [0]

            def inverse_root(b):
                uses[0] += 1
                pool.wait_ge(var_ready, uses[0])
                nc.gpsimd.tensor_tensor(rstd[:, b, :], var_eps[:, b, :], power[:, 0:TT],
                                        ALU.pow).then_inc(rstd_ready, 1)

            inverse_root(0)
            inverse_root(1)
            nc.gpsimd.memset(v_sb[:, :, :, HD:], 1.0 + PROB_EPS).then_inc(v_ones, 1)

            def cross_terms(b, t):
                pool.wait_ge(*taken("kv", b, t))
                if t == 0:
                    pool.wait_ge(loaded["sin"], 16)
                    if b > 0:
                        pool.wait_ge(prod_ready[b - 1], 2)
                for odd in range(2):
                    last = nc.gpsimd.tensor_tensor(
                        crossed[:, t, :, odd::2], kv[:, t, :, 1 - odd:ROT:2],
                        sin[:, t, odd::2].unsqueeze(1).to_broadcast([P, 2, ROT // 2]), ALU.mult)
                last.then_inc(crossed_ready[b], 1)

            def norms(b):
                pool.wait_ge(norms_ready[b], 2 * TT)
                link(nc.gpsimd.tensor_tensor(norm_inv[:, b], norm_sq[:, b],
                                             power[:].rearrange("p (a c) -> p a c", a=TT), ALU.pow))
                nc.gpsimd.tensor_tensor(pair_inv[:, b], norm_inv[:, b, :, 0], norm_inv[:, b, :, 1],
                                        ALU.mult).then_inc(pair_ready[b], 1)

            def low(hl, raw, high_ready, ready):
                pool.wait_ge(high_ready, 1)
                nc.gpsimd.tensor_tensor(hl[1][:], raw[:], hl[0][:], ALU.subtract).then_inc(ready, 1)

            def low_chunk(hl, raw, c, high_ready, ready):
                pool.wait_ge(high_ready, c + 1)
                nc.gpsimd.tensor_tensor(hl[1][:, c], raw[:, c], hl[0][:, c], ALU.subtract).then_inc(ready, 1)

            cross_terms(0, 0)
            cross_terms(0, 1)
            norms(0)
            low(wk_hl, wk_sb, wk_high_ready, wk_low_ready)
            cross_terms(1, 0)
            cross_terms(1, 1)
            norms(1)
            inverse_root(0)
            low(wv_hl, wv_sb, wv_high_ready, wv_low_ready)
            pool.wait_ge(ctx_high_ready[1], 1)
            nc.gpsimd.tensor_tensor(ctx_hl[1][:, :, T:], ctx_sb[:, :, T:], ctx_hl[0][:, :, T:],
                                    ALU.subtract).then_inc(ctx_low_ready[1], 1)
            low_chunk(gate_hl, gate_sb, 0, gate_high_ready, gate_low_ready)
            low_chunk(gate_hl, gate_sb, 1, gate_high_ready, gate_low_ready)
            pool.wait_ge(loaded["late_row"], 16)
            for f in range(0, FC, DOWN_RUN):
                pool.wait_ge(down_rows_scaled, f // DOWN_RUN + 1)
                nc.gpsimd.tensor_tensor(down_sb[:, f:f + DOWN_RUN], down_sb[:, f:f + DOWN_RUN],
                                        row[:, R_DS:R_DS + D].unsqueeze(1).to_broadcast([P, DOWN_RUN, D]),
                                        ALU.mult).then_inc(down_scaled, 1)
            inverse_root(1)
            for f in range(0, FC, DOWN_RUN):
                pool.wait_ge(down_high_ready, f // DOWN_RUN + 1)
                nc.gpsimd.tensor_tensor(down_hl[1][:, f:f + DOWN_RUN], down_sb[:, f:f + DOWN_RUN],
                                        down_hl[0][:, f:f + DOWN_RUN], ALU.subtract).then_inc(down_low_ready, 1)
            for b in range(B):
                pool.wait_ge(x1_ready[b], 2)
                nc.gpsimd.tensor_tensor(x1b[:, TT * b:TT * (b + 1)], x1[:, TT * b:TT * (b + 1)],
                                        row[:, R_LB:R_LB + D].unsqueeze(1).to_broadcast([P, TT, D]),
                                        ALU.add).then_inc(x1b_ready[b], 1)
            low_chunk(up_hl, up_sb, 0, up_high_ready, up_low_ready)
            low_chunk(up_hl, up_sb, 1, up_high_ready, up_low_ready)
            pool.wait_ge(res_ready, 2)

            def after_cross(b):
                uses[0] += 1
                pool.wait_ge(var_ready, uses[0])
                link(nc.gpsimd.tensor_tensor(rstd[:, b, :], var_eps[:, b, :], power[:, 0:TT], ALU.pow))
                ins = nc.gpsimd.tensor_tensor(rstd_rs[:, b, :], rstd[:, b, :], res2[:, 0:1].to_broadcast([P, TT]),
                                              ALU.mult)
                if b == 0:
                    link(ins)
                else:
                    ins.then_inc(rstd_ready, 1)

            def hidden_low(b, m):
                pool.wait_ge(hidden_high_ready, b * (FC // 2) + m + 1)
                n = b * (FC // 2) + m
                nc.gpsimd.tensor_tensor(hidden_hl[1][:, 2 * m:2 * m + 2], silu[:, n % 2],
                                        hidden_hl[0][:, 2 * m:2 * m + 2], ALU.subtract).then_inc(hidden_low_ready, 1)

            after_cross(0)
            pool.wait_ge(delta_centred, 1)
            link(nc.gpsimd.tensor_tensor(delta, delta, rstd_rs[:, 0].unsqueeze(2).to_broadcast([P, TT, D]), ALU.mult))
            nc.gpsimd.tensor_tensor(delta, delta, x1b[:, 0:TT], ALU.add).then_inc(delta_summed, 1)
            inverse_root(0)
            hidden_low(0, 0)
            after_cross(1)
            hidden_low(0, 1)
            inverse_root(1)
            inverse_root(0)
            for t in range(TT):
                uses[0] += 1
                pool.wait_ge(var_ready, uses[0])
                nc.gpsimd.tensor_tensor(rstd[:, 1, t:t + 1], var_eps[:, 1, t:t + 1], power[:, 0:1],
                                        ALU.pow).then_inc(rstd_ready, 1)

        @block.scalar
        def _(act):
            act.dma_start(col[:], cols).then_inc(loaded["col"], 16)
            act.dma_start(mask_sb[:], mask_cols).then_inc(loaded["mask"], 16)

            def k_first(b, c):
                act.wait_ge(*filled("k", b, c))
                if b > 0:
                    act.wait_ge(k_stored[b - 1][0], 16)
                nc.scalar.activation(k_part[0][:, c, :], ps[:, bank("k", b, c), :], ACT.Identity,
                                     bias=col[:, C_BK + c:C_BK + c + 1]).then_inc(k1_ready[b], 1)

            def k_second(b, c):
                act.wait_ge(*taken("k", b, c))
                if b > 0:
                    act.wait_ge(k_stored[b - 1][1], 16)
                nc.scalar.activation(k_part[1][:, c], k_rest[:, c], ACT.Copy).then_inc(k2_ready[b], 1)

            def q_first(b, chunks=range(DC)):
                if chunks[0] == 0:
                    act.wait_ge(*filled("q", b))
                    if b > 0:
                        act.wait_ge(q_stored[b - 1][0], 16)
                for c in chunks:
                    last = nc.scalar.activation(q_part[0][:, c, :], ps[:, bank("q", b), S * c:S * (c + 1)],
                                                ACT.Identity, bias=col[:, C_BQ + c:C_BQ + c + 1])
                if chunks[-1] == DC - 1:
                    last.then_inc(q1_ready[b], 1)

            def q_second(b):
                act.wait_ge(*taken("q", b))
                if b > 0:
                    act.wait_ge(q_stored[b - 1][1], 16)
                nc.scalar.activation(q_part[1][:], q_rest[:], ACT.Copy).then_inc(q2_ready[b], 1)

            def z_scale(b):
                act.wait_ge(*filled("zt", b, 0))
                nc.scalar.activation(z_t[:, 0, S * b:S * (b + 1)], ps[:, bank("zt", b, 0), 0:S],
                                     ACT.Identity, scale=col[:, C_GAMMA:C_GAMMA + 1],
                                     bias=col[:, C_BETA:C_BETA + 1]).then_inc(*take("zt", b, 0))

            def square_norms(b, t):
                if b > 0 and t == 0:
                    act.wait_ge(norms_ready[b - 1], 2 * TT)
                act.wait_ge(*taken("kv", b, t))
                for n in range(2):
                    nc.scalar.activation(squares[:, t, n, :], kv[:, t, n, :], ACT.Square,
                                         accum_out=norm_sq[:, b, t, n:n + 1]).then_inc(norms_ready[b], 1)

            def take_x1_t(b):
                act.wait_ge(*filled("x1t", b))
                nc.scalar.activation(x1_t[:, :, S * b:S * (b + 1)],
                                     ps[:, bank("x1t", b), :].rearrange("p (c s) -> p c s", c=DC),
                                     ACT.Copy).then_inc(*take("x1t", b))

            def high_by_chunk(hl, raw, name, ready):
                act.wait_ge(loaded[name], 16)
                for c in range(DC):
                    nc.scalar.activation(hl[0][:, c], raw[:, c], ACT.Copy).then_inc(ready, 1)

            def scale_rows(f0):
                for f in range(f0, f0 + DOWN_RUN):
                    last = nc.scalar.activation(down_sb[:, f], down_sb[:, f], ACT.Copy,
                                                scale=col[:, C_US + f:C_US + f + 1])
                last.then_inc(down_rows_scaled, 1)

            def down_high(f0):
                act.wait_ge(down_scaled, f0 // DOWN_RUN + 1)
                nc.scalar.activation(down_hl[0][:, f0:f0 + DOWN_RUN], down_sb[:, f0:f0 + DOWN_RUN],
                                     ACT.Copy).then_inc(down_high_ready, 1)

            def high(hl, raw, name, ready):
                act.wait_ge(loaded[name], 16)
                nc.scalar.activation(hl[0][:], raw[:], ACT.Copy).then_inc(ready, 1)

            def ctx_high(b):
                act.wait_ge(loaded[f"ctx{b}"], 16)
                nc.scalar.activation(ctx_hl[0][:, :, T * b:T * (b + 1)], ctx_sb[:, :, T * b:T * (b + 1)],
                                     ACT.Copy).then_inc(ctx_high_ready[b], 1)

            def take_pv(b, g):
                n = b * NG + g
                act.wait_ge(*filled("pv", b, g))
                act.wait_ge(*filled("pvt", *divmod(n - 2, NG)))
                nc.scalar.activation(pv_sb[:, n % 2, :], ps[:, bank("pv", b, g), 0:S],
                                     ACT.Copy).then_inc(*take("pv", b, g))

            def x2_high(b):
                act.wait_ge(*filled("x2t", b))
                if b > 0:
                    act.wait_ge(*filled("up", b - 1, FC // 2 - 1))
                nc.scalar.activation(x2_hl[0][:], ps[:, bank("x2t", b), :].rearrange("p (c s) -> p c s", c=DC),
                                     ACT.Copy).then_inc(x2_high_ready, 1)

            def hidden_high(b, m):
                act.wait_ge(*taken("up", b, m))
                if b > 0:
                    act.wait_ge(*filled("down", b - 1, TT - 1))
                n = b * (FC // 2) + m
                nc.scalar.activation(hidden_hl[0][:, 2 * m:2 * m + 2], silu[:, n % 2],
                                     ACT.Copy).then_inc(hidden_high_ready, 1)

            nc.scalar.preload_act_table(ACT.Exp)
            act.wait_ge(loaded["col"], 16)
            z_scale(0)
            square_norms(0, 0)
            z_scale(1)
            square_norms(0, 1)
            ctx_high(0)
            high(wk_hl, wk_sb, "wk", wk_high_ready)
            high(wv_hl, wv_sb, "wv", wv_high_ready)
            ctx_high(1)
            square_norms(1, 0)
            square_norms(1, 1)
            high_by_chunk(gate_hl, gate_sb, "gate", gate_high_ready)
            k_first(0, 0)
            take_x1_t(0)
            k_second(0, 0)
            k_first(0, 1)
            k_second(0, 1)
            q_first(0)
            act.wait_ge(loaded["down"], 16)
            scale_rows(0)
            q_second(0)
            scale_rows(DOWN_RUN)
            high_by_chunk(up_hl, up_sb, "up", up_high_ready)
            down_high(0)
            k_first(1, 0)
            down_high(DOWN_RUN)
            k_second(1, 0)
            k_first(1, 1)
            take_x1_t(1)
            k_second(1, 1)

            act.wait_ge(mask_ready, 1)
            for b in range(B):
                for s in range(STEPS):
                    kt = s % KT
                    e = exp_of(b, s)
                    act.wait_ge(*filled("scores", b, s))
                    if e > NE:
                        act.wait_ge(*used(e - NE - 1))
                    k0 = bank("scores", b, s)
                    nc.scalar.activation(weights[:, (e - 1) % NE],
                                         ps[:, k0:k0 + 2, :].rearrange("p a (h s) -> p (a h) s", h=2), ACT.Exp,
                                         scale=SCORE_SCALE, bias=mask_bias[:, b * KT + kt:b * KT + kt + 1]).then_inc(*take("scores", b, s))
                    if b == 0 and s == 1:
                        q_first(1, [0])
                    if b == 0 and s == 2:
                        q_first(1, [1])
                    if b == 0 and s == 6:
                        q_second(1)
                    if b > 0 and s % KT == 1:
                        take_pv(*divmod(b * NG + s // KT - 1, NG))
                    if b == 1 and s == STEPS - 1:
                        x2_high(0)

            nc.scalar.preload_act_table(ACT.Silu)
            act.wait_ge(k3_ready[1], DC)

            def silus(b, m):
                n = b * (FC // 2) + m
                act.wait_ge(*filled("gate", b, m))
                if n >= 2:
                    act.wait_ge(hidden_low_ready, n - 1)
                for i in range(2):
                    last = nc.scalar.activation(silu[:, n % 2, i, :], ps[:, bank("gate", b, m), S * i:S * (i + 1)],
                                                ACT.Silu, scale=col[:, C_GS + 2 * m + i:C_GS + 2 * m + i + 1])
                last.then_inc(*take("gate", b, m))

            for b in range(B):
                if b > 0:
                    x2_high(b)
                silus(b, 0)
                silus(b, 1)
                hidden_high(b, 0)
                hidden_high(b, 1)
                silus(b, 2)
                hidden_high(b, 2)

        @block.vector
        def _(dve):
            steps = [0]

            def link(ins):
                steps[0] += 1
                ins.then_inc(dve_step, 1)
                dve.wait_ge(dve_step, steps[0])

            roots, root_of = [0], [0] * B

            def moments(b, src, scale=1.0):
                for t in range(TT):
                    last = nc.vector.bn_stats(stats[:, b, t, :], src(t))
                link(last)
                for t in range(TT):
                    last = nc.vector.bn_aggr(mean_var[:, b, t, :], stats[:, b, t, :])
                link(last)
                nc.vector.tensor_scalar(var_eps[:, b, :], mean_var[:, b, :, 1], scale, EPS,
                                        ALU.mult, ALU.add).then_inc(var_ready, 1)
                roots[0] += 1
                root_of[b] = roots[0]

            def normalise(b, src, dst, ready, tiles=range(TT)):
                dve.wait_ge(rstd_ready, root_of[b])
                for t in tiles:
                    nc.vector.tensor_scalar(dst(t), src(t), mean_var[:, b, t, 0:1], rstd[:, b, t:t + 1],
                                            ALU.subtract, ALU.mult).then_inc(ready, 1)

            def z_scale(b):
                dve.wait_ge(*filled("zt", b, 1))
                nc.vector.tensor_scalar(z_t[:, 1, S * b:S * (b + 1)], ps[:, bank("zt", b, 1), 0:S],
                                        col[:, C_GAMMA + 1:C_GAMMA + 2], col[:, C_BETA + 1:C_BETA + 2],
                                        ALU.mult, ALU.add).then_inc(*take("zt", b, 1))

            for b in range(B):
                dve.wait_ge(loaded[f"x{b}"], 16)
                moments(b, lambda t: x_sb[:, TT * b + t, :])
                if b > 0:
                    dve.wait_ge(loaded["col"], 16)
                    z_scale(0)
                normalise(b, lambda t: x_sb[:, TT * b + t, :], lambda t: z[:, TT * b + t, :], z_ready[b])

            dve.wait_ge(loaded["mask"], 16)
            nc.vector.tensor_scalar(mask_bias[:], mask_sb[:], 0.5, MASKED, ALU.is_le, ALU.mult).then_inc(mask_ready, 1)
            dve.wait_ge(loaded["col"], 16)
            nc.vector.tensor_scalar(res2[:, 0:1], col[:, C_RS:C_RS + 1], 0.0, 0.3,
                                    ALU.max, ALU.min).then_inc(res_ready, 1)
            dve.wait_ge(res_ready, 1)
            nc.vector.tensor_tensor(res2[:, 1:2], res2[:, 0:1], res2[:, 0:1], ALU.mult).then_inc(res_ready, 1)

            def first_residual():
                dve.wait_ge(loaded["row"], 16)
                for t in range(B * TT):
                    last = nc.vector.scalar_tensor_tensor(out=x2b[:, t], in0=x_sb[:, t], scalar=2.0,
                                                          in1=row[:, R_BOUT:R_BOUT + D], op0=ALU.mult, op1=ALU.add)
                link(last)

            def ctx_low(b):
                dve.wait_ge(ctx_high_ready[b], 1)
                nc.vector.tensor_tensor(ctx_hl[1][:, :, T * b:T * (b + 1)], ctx_sb[:, :, T * b:T * (b + 1)],
                                        ctx_hl[0][:, :, T * b:T * (b + 1)], ALU.subtract).then_inc(ctx_low_ready[b], 1)

            def kv_bias(b, t):
                dve.wait_ge(*filled("kv", b, t))
                if b > 0 and t == 0:
                    dve.wait_ge(norms_ready[b - 1], 2 * TT)
                nc.vector.tensor_tensor(kv[:, t].rearrange("p a d -> p (a d)"), ps[:, bank("kv", b, t), :],
                                        row[:, R_BKV:R_BKV + 2 * D], ALU.add).then_inc(*take("kv", b, t))

            def cosine_terms(b, t):
                dve.wait_ge(*taken("kv", b, t))
                nc.vector.tensor_tensor(turned[:, t], kv[:, t, :, 0:ROT],
                                        cos[:, t].unsqueeze(1).to_broadcast([P, 2, ROT]), ALU.mult)
                if t == TT - 1:
                    nc.vector.tensor_tensor(kv_prod[:, b, :, ROT:], kv[:, :, 0, ROT:], kv[:, :, 1, ROT:],
                                            ALU.mult).then_inc(prod_ready[b], 1)

            def products(b):
                dve.wait_ge(prod_ready[b], 1)
                dve.wait_ge(crossed_ready[b], TT)
                link(nc.vector.tensor_tensor(turned[:], turned[:], crossed[:], ALU.add))
                nc.vector.tensor_tensor(kv_prod[:, b, :, 0:ROT], turned[:, :, 0, :], turned[:, :, 1, :],
                                        ALU.mult).then_inc(prod_ready[b], 1)

            def gate_queries(b):
                dve.wait_ge(*filled("a", b))
                nc.vector.tensor_scalar(gate_a[:, b, :], ps[:, bank("a", b), 0:DC], 0.5, 0.5,
                                        ALU.mult, ALU.add).then_inc(*take("a", b))
                dve.wait_ge(*taken("a", b))
                dve.wait_ge(*filled("aq", b))
                for c in range(DC):
                    last = nc.vector.tensor_scalar(aq_t[:, c, S * b:S * (b + 1)],
                                                   ps[:, bank("aq", b), S * c:S * (c + 1)],
                                                   col[:, C_BIN + c:C_BIN + c + 1], gate_a[:, b, c:c + 1],
                                                   ALU.add, ALU.mult)
                last.then_inc(*take("aq", b))

            def v_bias(b, n):
                dve.wait_ge(*filled("v", b, n))
                dve.wait_ge(v_ones, 1)
                for i in range(2):
                    kt = b * KT + 2 * n + i
                    last = nc.vector.tensor_tensor(
                        v_sb[:, kt, :, 0:HD],
                        ps[:, bank("v", b, n), D * i:D * (i + 1)].rearrange("p (h d) -> p h d", d=HD),
                        row[:, R_BV:R_BV + D].rearrange("p (h d) -> p h d", d=HD), ALU.add)
                last.then_inc(*take("v", b, n))

            def stream1_sum(b):
                h1 = x2b[:, TT * b:TT * (b + 1)]
                dve.wait_ge(*filled("y", b))
                nc.vector.tensor_tensor(h1, ps[:, bank("y", b), :].rearrange("p (t d) -> p t d", t=TT), h1,
                                        ALU.add).then_inc(*take("y", b))
                dve.wait_ge(*taken("y", b))
                moments(b, lambda t: x2b[:, TT * b + t, :])

            def stream1_norm(b):
                normalise(b, lambda t: x2b[:, TT * b + t, :], lambda t: x1[:, TT * b + t, :], x1_ready[b])

            def k_remainder(b, c):
                dve.wait_ge(k1_ready[b], c + 1)
                if b > 0:
                    dve.wait_ge(k3_ready[b - 1], c + 1)
                nc.vector.scalar_tensor_tensor(out=k_rest[:, c], in0=ps[:, bank("k", b, c), :],
                                               scalar=col[:, C_BK + c:C_BK + c + 1], in1=k_part[0][:, c],
                                               op0=ALU.add, op1=ALU.subtract).then_inc(*take("k", b, c))

            def k_third(b, c):
                dve.wait_ge(k2_ready[b], c + 1)
                if b > 0:
                    dve.wait_ge(k_stored[b - 1][2], 16)
                nc.vector.tensor_tensor(k_part[2][:, c], k_rest[:, c], k_part[1][:, c],
                                        ALU.subtract).then_inc(k3_ready[b], 1)

            def q_remainder(b, chunks=range(DC)):
                if chunks[0] == 0:
                    dve.wait_ge(q1_ready[b], 1)
                    if b > 0:
                        dve.wait_ge(q3_ready[b - 1], 1)
                for c in chunks:
                    last = nc.vector.scalar_tensor_tensor(out=q_rest[:, c],
                                                          in0=ps[:, bank("q", b), S * c:S * (c + 1)],
                                                          scalar=col[:, C_BQ + c:C_BQ + c + 1], in1=q_part[0][:, c],
                                                          op0=ALU.add, op1=ALU.subtract)
                if chunks[-1] == DC - 1:
                    last.then_inc(*take("q", b))

            def q_third(b):
                dve.wait_ge(q2_ready[b], 1)
                if b > 0:
                    dve.wait_ge(q_stored[b - 1][2], 16)
                nc.vector.tensor_tensor(q_part[2][:], q_rest[:], q_part[1][:],
                                        ALU.subtract).then_inc(q3_ready[b], 1)

            dve.wait_ge(loaded["cos"], 16)
            dve.wait_ge(loaded["row"], 16)
            first_residual()
            kv_bias(0, 0)
            cosine_terms(0, 0)
            kv_bias(0, 1)
            z_scale(1)
            cosine_terms(0, 1)
            products(0)
            ctx_low(0)
            kv_bias(1, 0)
            gate_queries(0)
            cosine_terms(1, 0)
            kv_bias(1, 1)
            cosine_terms(1, 1)
            stream1_sum(0)
            products(1)
            stream1_norm(0)
            k_remainder(0, 0)
            gate_queries(1)
            k_remainder(0, 1)
            k_third(0, 0)
            k_third(0, 1)
            q_remainder(0)
            q_third(0)
            stream1_sum(1)
            dve.wait_ge(loaded["late_row"], 16)
            v_bias(0, 0)
            v_bias(0, 1)
            stream1_norm(1)
            k_remainder(1, 0)
            k_third(1, 0)
            k_remainder(1, 1)
            k_third(1, 1)
            v_bias(1, 0)
            v_bias(1, 1)

            def take_pv(b, g):
                n = b * NG + g
                dve.wait_ge(*filled("pv", b, g))
                if n >= 2:
                    dve.wait_ge(*filled("pvt", *divmod(n - 2, NG)))
                nc.vector.tensor_copy(pv_sb[:, n % 2, :],
                                      ps[:, bank("pv", b, g), 0:S]).then_inc(*take("pv", b, g))

            def normalise_ctx(b, g):
                dve.wait_ge(*filled("pvt", b, g))
                t_view = ps[:, bank("pvt", b, g), 0:TT * P].rearrange("p (t h r) -> p t h r", t=TT, r=32)
                link(nc.vector.reciprocal(total_inv[:], t_view[:, :, :, HD]))
                for t in range(TT):
                    last = nc.vector.tensor_tensor(
                        ctx_out[:, t, g * HG * HD:(g + 1) * HG * HD].rearrange("p (h d) -> p h d", d=HD),
                        t_view[:, t, :, 0:HD], total_inv[:, t].unsqueeze(2).to_broadcast([P, HG, HD]), ALU.mult)
                last.then_inc(*take("pvt", b, g))

            def take_ctx(b, c):
                dve.wait_ge(*filled("ctxt", b, c))
                if b > 0:
                    dve.wait_ge(*filled("delta", b - 1))
                nc.vector.tensor_copy(ctx_out_t[:, c, :],
                                      ps[:, bank("ctxt", b, c), 0:S]).then_inc(*take("ctxt", b, c))

            def delta_moments(b):
                dve.wait_ge(*filled("delta", b))
                nc.vector.tensor_tensor(delta, ps[:, bank("delta", b), :].rearrange("p (t d) -> p t d", t=TT),
                                        row[:, R_BO:R_BO + D].unsqueeze(1).to_broadcast([P, TT, D]),
                                        ALU.add).then_inc(*take("delta", b))
                dve.wait_ge(*taken("delta", b))
                moments(b, lambda t: delta[:, t, :], scale=res2[:, 1:2])
                if b == 0:
                    roots[0] -= 1

            def delta_centre(b):
                for t in range(TT):
                    last = nc.vector.scalar_tensor_tensor(out=delta[:, t, :], in0=delta[:, t, :],
                                                          scalar=mean_var[:, b, t, 0:1], in1=row[:, R_LG:R_LG + D],
                                                          op0=ALU.subtract, op1=ALU.mult)
                if b == 0:
                    last.then_inc(delta_centred, 1)
                else:
                    link(last)

            def stream2_sum(b):
                if b == 0:
                    dve.wait_ge(delta_summed, 1)
                    return
                dve.wait_ge(rstd_ready, root_of[b])
                dve.wait_ge(x1b_ready[b], 1)
                for t in range(TT):
                    last = nc.vector.scalar_tensor_tensor(out=delta[:, t, :], in0=delta[:, t, :],
                                                          scalar=rstd_rs[:, b, t:t + 1], in1=x1b[:, TT * b + t],
                                                          op0=ALU.mult, op1=ALU.add)
                link(last)

            def stream2_moments(b):
                moments(b, lambda t: delta[:, t, :])

            def stream2_normalise(b):
                normalise(b, lambda t: delta[:, t, :], lambda t: x2[:, TT * b + t, :], x2_ready[b])

            dve.wait_ge(res_ready, 2)
            for b in range(B):
                for s in range(STEPS):
                    e = exp_of(b, s)
                    dve.wait_ge(*taken("scores", b, s))
                    w = weights[:, (e - 1) % NE].rearrange("p h s -> p (h s)")
                    nc.vector.tensor_scalar(w, w, E_HIGH, E_LOW, ALU.min, ALU.max).then_inc(clipped, 1)
                    if b == 0 and s == 3:
                        q_remainder(1, [0])
                    if b == 0 and s == 5:
                        q_remainder(1, [1])
                    if b == 0 and s == 7:
                        q_third(1)
                    g = s // KT - 1
                    if b == 0 and g >= 0 and s % KT == 0:
                        take_pv(b, g)
                    if g >= 0 and s % KT == 2:
                        normalise_ctx(b, g)
                    if s % KT == 0 and g == 2:
                        take_ctx(b, 0)
                    if b > 0 and s == 2:
                        normalise_ctx(b - 1, NG - 1)
                    if b > 0 and s == 4:
                        take_ctx(b - 1, 1)
                    if b > 0 and s == 7:
                        delta_moments(b - 1)
                    if b > 0 and s == 8:
                        delta_centre(b - 1)
                    if b > 0 and s == 11:
                        stream2_sum(b - 1)
                        stream2_moments(b - 1)
                    if b > 0 and s == 13:
                        stream2_normalise(b - 1)

            def x2_low(b):
                dve.wait_ge(x2_high_ready, b + 1)
                nc.vector.tensor_tensor(x2_hl[1][:], ps[:, bank("x2t", b), :].rearrange("p (c s) -> p c s", c=DC),
                                        x2_hl[0][:], ALU.subtract).then_inc(*take("x2t", b))

            def gated(b, m):
                dve.wait_ge(*filled("up", b, m))
                dve.wait_ge(*taken("gate", b, m))
                n = b * (FC // 2) + m
                nc.vector.tensor_tensor(silu[:, n % 2],
                                        ps[:, bank("up", b, m), :].rearrange("p (a s) -> p a s", a=2),
                                        silu[:, n % 2], ALU.mult).then_inc(*take("up", b, m))

            def hidden_low(b, m):
                n = b * (FC // 2) + m
                dve.wait_ge(hidden_high_ready, n + 1)
                nc.vector.tensor_tensor(hidden_hl[1][:, 2 * m:2 * m + 2], silu[:, n % 2],
                                        hidden_hl[0][:, 2 * m:2 * m + 2], ALU.subtract).then_inc(hidden_low_ready, 1)

            def output(b):
                dve.wait_ge(x2_ready[B - 1], TT)
                for t in range(TT):
                    dve.wait_ge(*filled("down", b, t))
                    nc.vector.tensor_tensor(delta[:, t, :], ps[:, bank("down", b, t), 0:D], x2[:, TT * b + t, :],
                                            ALU.add).then_inc(*take("down", b, t))
                for t in range(TT):
                    dve.wait_ge(*taken("down", b, t))
                moments(b, lambda t: delta[:, t, :])
                normalise(b, lambda t: delta[:, t, :], lambda t: final[:, TT * b + t, :], final_ready)

            x2_low(0)
            take_pv(1, NG - 1)
            normalise_ctx(1, NG - 1)
            take_ctx(1, 1)
            gated(0, 0)
            delta_moments(1)
            delta_centre(1)
            gated(0, 1)
            stream2_sum(1)
            stream2_moments(1)
            gated(0, 2)
            stream2_normalise(1)
            hidden_low(0, 2)
            x2_low(1)
            output(0)
            for m in range(FC // 2):
                gated(1, m)
                hidden_low(1, m)
            b = B - 1
            dve.wait_ge(final_ready, TT * b)
            for t in range(TT):
                dve.wait_ge(*filled("down", b, t))
                nc.vector.tensor_tensor(delta[:, t, :], ps[:, bank("down", b, t), 0:D], x2[:, TT * b + t, :],
                                        ALU.add).then_inc(*take("down", b, t))
                if t == 0:
                    dve.wait_ge(*taken("down", b, t))
                    nc.vector.bn_stats(stats[:, b, t, :], delta[:, t, :]).then_inc(last_stats, 1)
            dve.wait_ge(last_stats, 1)
            nc.vector.bn_aggr(mean_var[:, b, 0, :], stats[:, b, 0, :]).then_inc(last_mean, 1)
            dve.wait_ge(*taken("down", b, 1))
            nc.vector.bn_stats(stats[:, b, 1, :], delta[:, 1, :]).then_inc(last_stats, 1)
            for t in range(TT):
                dve.wait_ge(last_mean, t + 1)
                nc.vector.tensor_scalar(var_eps[:, b, t:t + 1], mean_var[:, b, t:t + 1, 1], 1.0, EPS,
                                        ALU.mult, ALU.add).then_inc(var_ready, 1)
                if t == 0:
                    dve.wait_ge(last_stats, 2)
                    nc.vector.bn_aggr(mean_var[:, b, 1, :], stats[:, b, 1, :]).then_inc(last_mean, 1)
            for t in range(TT):
                roots[0] += 1
                root_of[b] = roots[0]
                normalise(b, lambda t: delta[:, t, :], lambda t: final[:, TT * b + t, :], final_ready, tiles=[t])

        @block.tensor
        def _(pe):
            done = []

            def begin(*job):
                assert ORDER[len(done)] == job, (ORDER[len(done)], job)
                done.append(job)
                for earlier in PLAN.before[job]:
                    pe.wait_ge(*taken(*earlier))

            def transpose_z(b):
                for c in range(DC):
                    begin("zt", b, c)
                for t in range(TT):
                    pe.wait_ge(z_ready[b], t + 1)
                    for c in range(DC):
                        ins = nc.tensor.transpose(ps[:, bank("zt", b, c), P * t:P * (t + 1)],
                                                  z[:, TT * b + t, P * c:P * (c + 1)], ident[:])
                        if t == TT - 1:
                            ins.then_inc(*full("zt", b, c))

            def z_transposed(b):
                for c in range(DC):
                    pe.wait_ge(*taken("zt", b, c))

            def transposes(job, src, ready, need):
                begin(*job)
                pe.wait_ge(ready, need)
                for c in range(DC):
                    for t in range(TT):
                        last = nc.tensor.transpose(ps[:, bank(*job), S * c + P * t:S * c + P * (t + 1)],
                                                   src[:, TT * job[1] + t, P * c:P * (c + 1)], ident[:])
                last.then_inc(*full(*job))

            def split_product(dst, chunks, stationary, moving, first=True, end=True):
                chunks = list(chunks)
                terms = [(i, pair) for i in chunks for pair in HL_PAIRS]
                for n, (i, (u, w)) in enumerate(terms):
                    last = nc.tensor.matmul(dst, stationary(u, i), moving(w, i), start=(first and n == 0),
                                            stop=(end and n == len(terms) - 1))
                return last

            def k_proj(b, c):
                begin("k", b, c)
                split_product(ps[:, bank("k", b, c), :], range(DC), lambda u, i: wk_hl[u][:, i, P * c:P * (c + 1)],
                              lambda w, i: ctx_hl[w][:, i, T * b:T * (b + 1)]).then_inc(*full("k", b, c))

            def v_proj(b, n):
                begin("v", b, n)
                offset = T * b + S * n
                for t in range(TT):
                    last = split_product(ps[:, bank("v", b, n), D * t:D * (t + 1)], range(DC),
                                         lambda u, i: ctx_hl[u][:, i, offset + P * t:offset + P * (t + 1)],
                                         lambda w, i: wv_hl[w][:, i, :])
                last.then_inc(*full("v", b, n))

            def kv_proj(b, t):
                begin("kv", b, t)
                n = TT * b + t
                for i in range(DC):
                    last = nc.tensor.matmul(ps[:, bank("kv", b, t), :], z_t[:, i, P * n:P * (n + 1)],
                                            w_in_sb[:, i, D:3 * D], start=(i == 0), stop=(i == DC - 1))
                last.then_inc(*full("kv", b, t))

            def feature_proj(job, w, src):
                b = job[1]
                begin(*job)
                for c in range(DC):
                    for i in range(DC):
                        last = nc.tensor.matmul(ps[:, bank(*job), S * c:S * (c + 1)], w[:, i, P * c:P * (c + 1)],
                                                src[:, i, S * b:S * (b + 1)], start=(i == 0), stop=(i == DC - 1))
                last.then_inc(*full(*job))

            def token_proj(job, w, src, offset):
                begin(*job)
                for t in range(TT):
                    for i in range(DC):
                        last = nc.tensor.matmul(ps[:, bank(*job), D * t:D * (t + 1)],
                                                src[:, i, offset + P * t:offset + P * (t + 1)], w[:, i, :],
                                                start=(i == 0), stop=(i == DC - 1))
                last.then_inc(*full(*job))

            def similarity(b):
                begin("a", b)
                pe.wait_ge(prod_ready[b], 2)
                pe.wait_ge(pair_ready[b], 1)
                for c in range(DC):
                    for t in range(TT):
                        last = nc.tensor.matmul(ps[:, bank("a", b), c:c + 1], kv_prod[:, b, t, P * c:P * (c + 1)],
                                                pair_inv[:, b, t:t + 1], start=(t == 0), stop=(t == TT - 1))
                last.then_inc(*full("a", b))

            def y_proj(b):
                pe.wait_ge(*taken("aq", b))
                token_proj(("y", b), w_out_sb, aq_t, S * b)

            def q_proj(b):
                pe.wait_ge(*taken("x1t", b))
                feature_proj(("q", b), wq_sb, x1_t)

            pe.wait_ge(ident_ready, 1)
            for _ in range(WARM_UP):
                nc.tensor.transpose(ps[:, 7, 0:P], ident[:], ident[:])
            transpose_z(0)
            pe.wait_ge(loaded["w_kv"], 16)
            z_transposed(0)
            kv_proj(0, 0)
            kv_proj(0, 1)
            transpose_z(1)
            pe.wait_ge(loaded["w_q"], 16)
            feature_proj(("aq", 0), w_in_sb, z_t)
            z_transposed(1)
            kv_proj(1, 0)
            similarity(0)
            kv_proj(1, 1)
            pe.wait_ge(loaded["w_out"], 16)
            y_proj(0)
            feature_proj(("aq", 1), w_in_sb, z_t)
            pe.wait_ge(wk_low_ready, 1)
            pe.wait_ge(ctx_low_ready[0], 1)
            k_proj(0, 0)
            similarity(1)
            transposes(("x1t", 0), x1, x1_ready[0], 2)
            k_proj(0, 1)
            pe.wait_ge(loaded["wq"], 16)
            q_proj(0)
            y_proj(1)
            pe.wait_ge(wv_low_ready, 1)
            v_proj(0, 0)
            v_proj(0, 1)
            pe.wait_ge(ctx_low_ready[1], 1)
            k_proj(1, 0)
            k_proj(1, 1)
            v_proj(1, 0)
            v_proj(1, 1)
            transposes(("x1t", 1), x1, x1_ready[1], 2)

            def scores(b, s):
                g, kt = divmod(s, KT)
                begin("scores", b, s)
                if s == 0:
                    pe.wait_ge(stacked_first[b], 16 * 5)
                if s == KT:
                    pe.wait_ge(stacked_rest[b], 16 * 5)
                k0 = bank("scores", b, s)
                for j in range(HG):
                    h = g * HG + j
                    last = nc.tensor.matmul(ps[:, k0 + j // 2, S * (j % 2):S * (j % 2 + 1)],
                                            k_stack[b][:, h, P * kt:P * (kt + 1)],
                                            q_stack[b][:, h, :], start=True, stop=True)
                last.then_inc(*full("scores", b, s))

            def weigh(b, s):
                g, kt = divmod(s, KT)
                e = exp_of(b, s)
                if kt == 0:
                    begin("pv", b, g)
                pe.wait_ge(clipped, e)
                for j in range(HG):
                    last = nc.tensor.matmul(ps[32 * j:32 * (j + 1), bank("pv", b, g), 0:S],
                                            v_sb[:, b * KT + kt, g * HG + j, :], weights[:, (e - 1) % NE, j, :],
                                            start=(kt == 0), stop=(kt == KT - 1))
                last.then_inc(*(full("pv", b, g) if kt == KT - 1 else (weights_used, 1)))

            def transpose_pv(b, g):
                n = b * NG + g
                begin("pvt", b, g)
                pe.wait_ge(*taken("pv", b, g))
                for t in range(TT):
                    last = nc.tensor.transpose(ps[:, bank("pvt", b, g), P * t:P * (t + 1)],
                                               pv_sb[:, n % 2, P * t:P * (t + 1)], ident[:])
                last.then_inc(*full("pvt", b, g))

            def transpose_ctx(b, c):
                begin("ctxt", b, c)
                pe.wait_ge(*taken("pvt", b, 2 * c))
                pe.wait_ge(*taken("pvt", b, 2 * c + 1))
                for t in range(TT):
                    last = nc.tensor.transpose(ps[:, bank("ctxt", b, c), P * t:P * (t + 1)],
                                               ctx_out[:, t, P * c:P * (c + 1)], ident[:])
                last.then_inc(*full("ctxt", b, c))

            def out_proj(b):
                pe.wait_ge(*taken("ctxt", b, 0))
                pe.wait_ge(*taken("ctxt", b, 1))
                token_proj(("delta", b), wo_sb, ctx_out_t, 0)

            follow = {"pvt": transpose_pv, "ctxt": transpose_ctx, "delta": out_proj,
                      "x2t": lambda b: transposes(("x2t", b), x2, x2_ready[b], 2)}
            pe.wait_ge(loaded["wo"], 16)
            scores(0, 0)
            scores(0, 1)
            q_proj(1)
            for b in range(B):
                pe.wait_ge(*taken("v", b, 0))
                pe.wait_ge(*taken("v", b, 1))
                for s in range(STEPS):
                    if s + 2 < STEPS:
                        scores(b, s + 2)
                    elif b + 1 < B:
                        scores(b + 1, s + 2 - STEPS)
                    weigh(b, s)
                    for job in after_weigh(b, s):
                        follow[job[0]](*job[1:])

            def inner(kind, hl, b, m):
                begin(kind, b, m)
                for i in range(2):
                    f = 2 * m + i
                    last = split_product(ps[:, bank(kind, b, m), S * i:S * (i + 1)], range(DC),
                                         lambda u, c: hl[u][:, c, P * f:P * (f + 1)],
                                         lambda w, c: x2_hl[w][:, c, :])
                last.then_inc(*full(kind, b, m))

            def down(b, t, chunks):
                if chunks[0] == 0:
                    begin("down", b, t)
                pe.wait_ge(hidden_low_ready, b * (FC // 2) + chunks[-1] // 2 + 1)
                last = split_product(ps[:, bank("down", b, t), 0:D], chunks,
                                     lambda u, f: hidden_hl[u][:, f, P * t:P * (t + 1)],
                                     lambda w, f: down_hl[w][:, f, :], first=(chunks[0] == 0),
                                     end=(chunks[-1] == FC - 1))
                if chunks[-1] == FC - 1:
                    last.then_inc(*full("down", b, t))

            pe.wait_ge(gate_low_ready, DC)
            pe.wait_ge(up_low_ready, DC)
            pe.wait_ge(*taken("x2t", 0))
            first_chunks, next_chunks, last_chunks = (range(f, f + 2) for f in range(0, FC, 2))
            inner("gate", gate_hl, 0, 0)
            transpose_pv(1, NG - 1)
            inner("gate", gate_hl, 0, 1)
            transpose_ctx(1, 1)
            inner("up", up_hl, 0, 0)
            out_proj(1)
            inner("up", up_hl, 0, 1)
            inner("gate", gate_hl, 0, 2)
            inner("up", up_hl, 0, 2)
            pe.wait_ge(down_low_ready, FC // DOWN_RUN)
            down(0, 0, first_chunks)
            down(0, 1, first_chunks)
            down(0, 0, next_chunks)
            down(0, 1, next_chunks)
            transposes(("x2t", 1), x2, x2_ready[1], 2)
            down(0, 0, last_chunks)
            down(0, 1, last_chunks)
            pe.wait_ge(*taken("x2t", 1))
            inner("gate", gate_hl, 1, 0)
            inner("gate", gate_hl, 1, 1)
            inner("up", up_hl, 1, 0)
            inner("up", up_hl, 1, 1)
            inner("gate", gate_hl, 1, 2)
            inner("up", up_hl, 1, 2)
            down(1, 0, first_chunks)
            down(1, 0, next_chunks)
            down(1, 1, first_chunks)
            down(1, 1, next_chunks)
            down(1, 0, last_chunks)
            down(1, 1, last_chunks)


def kernel(x, ctx_2048, mask_BxS2_ik0, L0_attn_W_in, L0_attn_b_in, L0_attn_W_out, L0_attn_b_out,
           L0_attn_gamma, L0_attn_beta, L0_xattn_Wq, L0_xattn_bq, L0_xattn_Wk, L0_xattn_bk, L0_xattn_Wv,
           L0_xattn_bv, L0_xattn_Wo, L0_xattn_bo, L0_xattn_ln_gamma, L0_xattn_ln_beta,
           L0_xattn_residual_scale, L0_ffn_gate_w, L0_ffn_up_w, L0_ffn_down_w, L0_ffn_gate_s,
           L0_ffn_up_s, L0_ffn_down_s):
    import concourse.bacc as bacc
    from concourse.bass_utils import run_bass_kernel_spmd

    f32 = np.float32

    def chunked(a):
        return np.asarray(a).reshape(-1, P).T

    def padded(a):
        a = np.asarray(a)
        return np.concatenate([a, np.zeros((FC * P - a.shape[0],) + a.shape[1:], a.dtype)])

    def heads_paired(a):
        a = np.asarray(a)
        return a.reshape(NH // DC, DC, HD, -1).transpose(1, 0, 2, 3).reshape(a.shape)

    cols = np.concatenate([chunked(L0_attn_gamma), chunked(L0_attn_beta), chunked(np.asarray(L0_attn_b_in)[:D]),
                           chunked(heads_paired(L0_xattn_bq)), chunked(heads_paired(L0_xattn_bk)),
                           chunked(padded(L0_ffn_gate_s)), chunked(padded(L0_ffn_up_s)),
                           np.broadcast_to(np.asarray(L0_xattn_residual_scale), (P, 1))], axis=1)
    rows = np.concatenate([np.asarray(a) for a in (
        np.asarray(L0_attn_b_in)[D:], L0_attn_b_out, L0_xattn_bv, L0_xattn_bo, L0_xattn_ln_gamma,
        L0_xattn_ln_beta, L0_ffn_down_s)])[None]
    inv_freq = f32(1.0) / f32(10000.0) ** (np.arange(0, ROT, 2, dtype=f32) / f32(ROT))
    angle = np.repeat(np.arange(S, dtype=f32)[:, None] * inv_freq[None, :], 2, axis=1)
    sign = np.tile(np.array([-1.0, 1.0], f32), ROT // 2)
    arrays = {
        "x": np.asarray(x).reshape(B * S, D),
        "ctx_t": np.asarray(ctx_2048).reshape(B * T, D).T,
        "mask_cols": np.asarray(mask_BxS2_ik0).reshape(B * KT, P).T,
        "cols": cols,
        "rows": rows,
        "rope_cos": np.cos(angle).astype(f32),
        "rope_sin": (np.sin(angle) * sign).astype(f32),
        "w_in": np.asarray(L0_attn_W_in),
        "w_out": np.asarray(L0_attn_W_out),
        "wq_t": heads_paired(L0_xattn_Wq).T,
        "wk_t": heads_paired(L0_xattn_Wk).T,
        "wv_t": np.asarray(L0_xattn_Wv).T,
        "wo_t": np.asarray(L0_xattn_Wo).T,
        "gate_t": padded(L0_ffn_gate_w).T,
        "up_t": padded(L0_ffn_up_w).T,
        "down_t": padded(np.asarray(L0_ffn_down_w).T),
    }
    arrays = {name: np.ascontiguousarray(a) for name, a in arrays.items()}

    nc = bacc.Bacc("TRN2", target_bir_lowering=False, num_devices=1)
    args = [nc.dram_tensor(name, a.shape, mybir.dt.from_np(a.dtype), kind="ExternalInput").ap()
            for name, a in arrays.items()]
    out = nc.dram_tensor("out", (B * S, D), F32, kind="ExternalOutput").ap()
    decoder_layer(nc, *args, out)
    result = run_bass_kernel_spmd(nc, [arrays], core_ids=[0])
    return result.results[0]["out"].reshape(B, S, D)
```
